# Optimizing a Trainium2 kernel written in Bass

```python
import numpy as np
import jax
import jax.numpy as jnp

def _softmax(x, axis=-1):
    return jax.nn.softmax(x, axis=axis)

def _gelu(x):
    return jax.nn.gelu(x, approximate=True)

def _silu(x):
    return jax.nn.silu(x)

def _sigmoid(x):
    return jax.nn.sigmoid(x)

def _layernorm(x, axis=-1, eps=1e-05):
    m = jnp.mean(x, axis=axis, keepdims=True)
    v = jnp.var(x, axis=axis, keepdims=True)
    return (x - m) / jnp.sqrt(v + eps)

def _scatter_add(tgt, idx, src, axis=0):
    return tgt.at[idx].add(src)

def _segment_sum(src, seg, n):
    return jax.ops.segment_sum(src, seg, n)
kernel_name = 'mk_seq_postln_d2_jaxref_r8_8f329f'

def setup_inputs(seed: int=0):
    np.random.seed(seed)
    _w = jnp.asarray

    def _L0_attn_setup():
        import jax, jax.numpy as jnp
        import numpy as np
        B, N, E, H = (1, 512, 256, 16)
        D = E // H
        DEGREE = 4
        LN_EPS = 1e-05
        ROPE_BASE = 10000.0

        def rope_cos_sin(n, d):
            inv_freq = 1.0 / ROPE_BASE ** (jnp.arange(0, d, 2, dtype=jnp.float32) / d)
            t = jnp.arange(n, dtype=jnp.float32)[:, None] * inv_freq[None, :]
            return (jnp.cos(t), jnp.sin(t))

        def apply_rope(x, cos, sin):
            x1, x2 = jnp.split(x, 2, axis=-1)
            c = cos[None, :, None, :]
            s = sin[None, :, None, :]
            return jnp.concatenate([x1 * c - x2 * s, x1 * s + x2 * c], axis=-1)

        def layernorm(x, scale, bias, eps=LN_EPS):
            m = jnp.mean(x, axis=-1, keepdims=True)
            v = jnp.var(x, axis=-1, keepdims=True)
            return (x - m) * jax.lax.rsqrt(v + eps) * scale + bias

        def polynomial_attention(q, k, v, degree, is_causal):
            a = jnp.einsum('bhnd,bhmd->bhnm', q, k) ** degree
            if is_causal:
                a = jnp.tril(a)
            denom = jnp.sum(a, axis=-1, keepdims=True)
            return jnp.einsum('bhnm,bhmd->bhnd', a / denom, v)
        key = jax.random.key(seed)
        k0, k1, k2 = jax.random.split(key, 3)
        x = jax.random.normal(k0, (B, N, E), dtype=jnp.float32)
        w_qkv = jax.random.normal(k1, (E, 3 * E), dtype=jnp.float32) * (1.0 / np.sqrt(E))
        w_out = jax.random.normal(k2, (E, E), dtype=jnp.float32) * (1.0 / np.sqrt(E))
        ln_scale = jnp.ones((D,), dtype=jnp.float32)
        ln_bias = jnp.zeros((D,), dtype=jnp.float32)
        return {'x': x, 'w_qkv': w_qkv, 'w_out': w_out, 'ln_scale': ln_scale, 'ln_bias': ln_bias}
    _L0_attn_in = _L0_attn_setup()

    def _L0_ffn_setup():
        import jax, jax.numpy as jnp
        import numpy as np
        B, S, D, FF, E = (4, 256, 256, 1024, 2)
        key = jax.random.key(seed)
        k0, k1, k2, k3, k4 = jax.random.split(key, 5)
        s = 0.02
        return {'hidden_states': jax.random.normal(k0, (B, S, D), jnp.float32), 'gate_w': jax.random.normal(k1, (E, D), jnp.float32) * s, 'w_gate': jax.random.normal(k2, (E, FF, D), jnp.float32) * s, 'w_up': jax.random.normal(k3, (E, FF, D), jnp.float32) * s, 'w_down': jax.random.normal(k4, (E, D, FF), jnp.float32) * s}
    _L0_ffn_in = _L0_ffn_setup()

    def _L1_attn_setup():
        import jax, jax.numpy as jnp
        import numpy as np
        import math
        FRAME_SIZE = 72
        GAMMA = 0.5
        NUM_HEADS = 32

        def rotate_half(x):
            x1, x2 = jnp.split(x, 2, axis=-1)
            return jnp.concatenate([-x2, x1], axis=-1)

        def apply_rope(x, freqs):
            return x * jnp.cos(freqs) + rotate_half(x) * jnp.sin(freqs)

        def rope_freqs(length, dim):
            theta = 10000.0 ** (-jnp.arange(0, dim, 2, dtype=jnp.float32) / dim)
            f = jnp.arange(length, dtype=jnp.float32)[:, None] * theta[None, :]
            return jnp.concatenate([f, f], axis=-1)
        key = jax.random.key(seed)
        ks = jax.random.split(key, 9)
        B, T, C = (2, 256, 256)
        s = 0.02
        return {'hidden_states': jax.random.normal(ks[0], (B, T, C), jnp.float32), 'Wq': jax.random.normal(ks[1], (C, C), jnp.float32) * s, 'bq': jnp.zeros((C,), jnp.float32), 'Wk': jax.random.normal(ks[2], (C, C), jnp.float32) * s, 'bk': jnp.zeros((C,), jnp.float32), 'Wv': jax.random.normal(ks[3], (C, C), jnp.float32) * s, 'bv': jnp.zeros((C,), jnp.float32), 'Wo': jax.random.normal(ks[4], (C, C), jnp.float32) * s, 'bo': jnp.zeros((C,), jnp.float32)}
    _L1_attn_in = _L1_attn_setup()

    def _L1_ffn_setup():
        import jax, jax.numpy as jnp
        import numpy as np
        HID = 256
        N_EXP = 32
        F_EXP = 96
        TOP_K = 6
        F_SH = 192
        B, S = (1, 128)
        key = jax.random.key(seed)
        ks = jax.random.split(key, 8)
        s = 0.02
        return {'hidden_states': jax.random.normal(ks[0], (B, S, HID), dtype=jnp.float32), 'gate_w': jax.random.normal(ks[1], (HID, N_EXP), dtype=jnp.float32) * s, 'wg': jax.random.normal(ks[2], (N_EXP, HID, F_EXP), dtype=jnp.float32) * s, 'wu': jax.random.normal(ks[3], (N_EXP, HID, F_EXP), dtype=jnp.float32) * s, 'wd': jax.random.normal(ks[4], (N_EXP, F_EXP, HID), dtype=jnp.float32) * s, 'sg': jax.random.normal(ks[5], (HID, F_SH), dtype=jnp.float32) * s, 'su': jax.random.normal(ks[6], (HID, F_SH), dtype=jnp.float32) * s, 'sd': jax.random.normal(ks[7], (F_SH, HID), dtype=jnp.float32) * s}
    _L1_ffn_in = _L1_ffn_setup()
    _d = {'L0_attn_x': _L0_attn_in['x'], 'L0_attn_w_qkv': _L0_attn_in['w_qkv'], 'L0_attn_w_out': _L0_attn_in['w_out'], 'L0_attn_ln_scale': _L0_attn_in['ln_scale'], 'L0_attn_ln_bias': _L0_attn_in['ln_bias'], 'L0_ffn_gate_w': _L0_ffn_in['gate_w'], 'L0_ffn_w_gate': _L0_ffn_in['w_gate'], 'L0_ffn_w_up': _L0_ffn_in['w_up'], 'L0_ffn_w_down': _L0_ffn_in['w_down'], 'L1_attn_Wq': _L1_attn_in['Wq'], 'L1_attn_bq': _L1_attn_in['bq'], 'L1_attn_Wk': _L1_attn_in['Wk'], 'L1_attn_bk': _L1_attn_in['bk'], 'L1_attn_Wv': _L1_attn_in['Wv'], 'L1_attn_bv': _L1_attn_in['bv'], 'L1_attn_Wo': _L1_attn_in['Wo'], 'L1_attn_bo': _L1_attn_in['bo'], 'L1_ffn_gate_w': _L1_ffn_in['gate_w'], 'L1_ffn_wg': _L1_ffn_in['wg'], 'L1_ffn_wu': _L1_ffn_in['wu'], 'L1_ffn_wd': _L1_ffn_in['wd'], 'L1_ffn_sg': _L1_ffn_in['sg'], 'L1_ffn_su': _L1_ffn_in['su'], 'L1_ffn_sd': _L1_ffn_in['sd']}
    _x0 = _d['L0_attn_x']
    _d['L0_attn_x'] = jax.random.normal(jax.random.fold_in(jax.random.key(seed), 1), (2, 1024, 256), dtype=_x0.dtype)
    del _x0
    return _d

def reference(L0_attn_x, L0_attn_w_qkv, L0_attn_w_out, L0_attn_ln_scale, L0_attn_ln_bias, L0_ffn_gate_w, L0_ffn_w_gate, L0_ffn_w_up, L0_ffn_w_down, L1_attn_Wq, L1_attn_bq, L1_attn_Wk, L1_attn_bk, L1_attn_Wv, L1_attn_bv, L1_attn_Wo, L1_attn_bo, L1_ffn_gate_w, L1_ffn_wg, L1_ffn_wu, L1_ffn_wd, L1_ffn_sg, L1_ffn_su, L1_ffn_sd):

    def _L0_attn_ref(x, w_qkv, w_out, ln_scale, ln_bias):
        import jax, jax.numpy as jnp
        import numpy as np
        B, N, E, H = (1, 512, 256, 16)
        D = E // H
        DEGREE = 4
        LN_EPS = 1e-05
        ROPE_BASE = 10000.0

        def rope_cos_sin(n, d):
            inv_freq = 1.0 / ROPE_BASE ** (jnp.arange(0, d, 2, dtype=jnp.float32) / d)
            t = jnp.arange(n, dtype=jnp.float32)[:, None] * inv_freq[None, :]
            return (jnp.cos(t), jnp.sin(t))

        def apply_rope(x, cos, sin):
            x1, x2 = jnp.split(x, 2, axis=-1)
            c = cos[None, :, None, :]
            s = sin[None, :, None, :]
            return jnp.concatenate([x1 * c - x2 * s, x1 * s + x2 * c], axis=-1)

        def layernorm(x, scale, bias, eps=LN_EPS):
            m = jnp.mean(x, axis=-1, keepdims=True)
            v = jnp.var(x, axis=-1, keepdims=True)
            return (x - m) * jax.lax.rsqrt(v + eps) * scale + bias

        def polynomial_attention(q, k, v, degree, is_causal):
            a = jnp.einsum('bhnd,bhmd->bhnm', q, k) ** degree
            if is_causal:
                a = jnp.tril(a)
            denom = jnp.sum(a, axis=-1, keepdims=True)
            return jnp.einsum('bhnm,bhmd->bhnd', a / denom, v)
        b, n, e = x.shape
        proj = x @ w_qkv
        q, k, v = jnp.split(proj, 3, axis=-1)
        q = q.reshape(b, n, H, D)
        k = k.reshape(b, n, H, D)
        v = v.reshape(b, n, H, D)
        cos, sin = rope_cos_sin(n, D)
        q = apply_rope(q, cos, sin)
        k = apply_rope(k, cos, sin)
        q = q.transpose(0, 2, 1, 3)
        k = k.transpose(0, 2, 1, 3)
        v = v.transpose(0, 2, 1, 3)
        q = layernorm(q, ln_scale, ln_bias)
        k = layernorm(k, ln_scale, ln_bias)
        out = polynomial_attention(q, k, v, DEGREE, True)
        out = out.transpose(0, 2, 1, 3).reshape(b, n, e)
        out = out @ w_out
        return out

    def _L0_ffn_ref(hidden_states, gate_w, w_gate, w_up, w_down):
        import jax, jax.numpy as jnp
        import numpy as np
        B, S, D, FF, E = (4, 256, 256, 1024, 2)
        b, s, d = hidden_states.shape
        x = hidden_states.reshape(-1, d)
        logits = x @ gate_w.T
        probs = jax.nn.softmax(logits.astype(jnp.float32), axis=-1)
        sel = jnp.argmax(probs, axis=-1)
        top_w = jnp.take_along_axis(probs, sel[:, None], axis=-1)
        onehot = jax.nn.one_hot(sel, gate_w.shape[0], dtype=x.dtype)
        g = jnp.einsum('td,efd->etf', x, w_gate)
        u = jnp.einsum('td,efd->etf', x, w_up)
        h = jax.nn.silu(g) * u
        y = jnp.einsum('etf,edf->etd', h, w_down)
        out = jnp.einsum('etd,te->td', y, onehot * top_w)
        return out.reshape(b, s, d)

    def _L1_attn_ref(hidden_states, Wq, bq, Wk, bk, Wv, bv, Wo, bo):
        import jax, jax.numpy as jnp
        import numpy as np
        import math
        FRAME_SIZE = 72
        GAMMA = 0.5
        NUM_HEADS = 32

        def rotate_half(x):
            x1, x2 = jnp.split(x, 2, axis=-1)
            return jnp.concatenate([-x2, x1], axis=-1)

        def apply_rope(x, freqs):
            return x * jnp.cos(freqs) + rotate_half(x) * jnp.sin(freqs)

        def rope_freqs(length, dim):
            theta = 10000.0 ** (-jnp.arange(0, dim, 2, dtype=jnp.float32) / dim)
            f = jnp.arange(length, dtype=jnp.float32)[:, None] * theta[None, :]
            return jnp.concatenate([f, f], axis=-1)
        B, T, C = hidden_states.shape
        H = NUM_HEADS
        dh = C // H

        def split_heads(x):
            return x.reshape(B, T, H, dh).transpose(0, 2, 1, 3)
        q = split_heads(hidden_states @ Wq.T + bq)
        k = split_heads(hidden_states @ Wk.T + bk)
        v = split_heads(hidden_states @ Wv.T + bv)
        freqs_abs = rope_freqs(T, dh)[None, None]
        q = apply_rope(q, freqs_abs)
        k = apply_rope(k, freqs_abs)
        temporal_ids = jnp.floor((jnp.arange(T) // FRAME_SIZE).astype(jnp.float32) * GAMMA).astype(jnp.int32)
        n_temp = int(math.floor((T - 1) // FRAME_SIZE * GAMMA)) + 1
        freqs_temp = rope_freqs(n_temp, dh)[temporal_ids][None, None]
        q = apply_rope(q, freqs_temp)
        k = apply_rope(k, freqs_temp)
        scores = jnp.einsum('bhqd,bhkd->bhqk', q, k) / math.sqrt(dh)
        causal = jnp.tril(jnp.ones((T, T), dtype=bool))
        scores = jnp.where(causal[None, None], scores, -jnp.inf)
        weights = jax.nn.softmax(scores, axis=-1)
        out = jnp.einsum('bhqk,bhkd->bhqd', weights, v)
        out = out.transpose(0, 2, 1, 3).reshape(B, T, H * dh)
        return out @ Wo.T + bo

    def _L1_ffn_ref(hidden_states, gate_w, wg, wu, wd, sg, su, sd):
        import jax, jax.numpy as jnp
        import numpy as np
        HID = 256
        N_EXP = 32
        F_EXP = 96
        TOP_K = 6
        F_SH = 192
        B, S = (1, 128)
        orig_shape = hidden_states.shape
        x = hidden_states.reshape(-1, HID)
        scores = jax.nn.sigmoid(x @ gate_w)
        topk_w, topk_i = jax.lax.top_k(scores, TOP_K)
        topk_w = topk_w / (jnp.sum(topk_w, axis=-1, keepdims=True) + 1e-20)
        combine = jnp.sum(jax.nn.one_hot(topk_i, N_EXP, dtype=topk_w.dtype) * topk_w[..., None], axis=1)
        g = jnp.einsum('td,edf->tef', x, wg)
        u = jnp.einsum('td,edf->tef', x, wu)
        act = jax.nn.silu(g) * u
        routed = jnp.einsum('tef,efd,te->td', act, wd, combine)
        routed = routed.reshape(orig_shape)
        shared = jax.nn.silu(hidden_states @ sg) * (hidden_states @ su) @ sd
        return routed + shared
    x = L0_attn_x
    x = _layernorm(x + _L0_attn_ref(x, L0_attn_w_qkv, L0_attn_w_out, L0_attn_ln_scale, L0_attn_ln_bias), axis=-1)
    x = _layernorm(x + _L0_ffn_ref(x, L0_ffn_gate_w, L0_ffn_w_gate, L0_ffn_w_up, L0_ffn_w_down), axis=-1)
    x = _layernorm(x + _L1_attn_ref(x, L1_attn_Wq, L1_attn_bq, L1_attn_Wk, L1_attn_bk, L1_attn_Wv, L1_attn_bv, L1_attn_Wo, L1_attn_bo), axis=-1)
    x = _layernorm(x + _L1_ffn_ref(x, L1_ffn_gate_w, L1_ffn_wg, L1_ffn_wu, L1_ffn_wd, L1_ffn_sg, L1_ffn_su, L1_ffn_sd), axis=-1)
    return x

_drawn_inputs = setup_inputs


def setup_inputs(seed=0):
    import zlib

    import numpy as np

    out = dict(_drawn_inputs(seed))
    spreads = {'L0_attn_ln_scale': (1.0, 0.2),
     'L0_attn_ln_bias': (0.0, 0.281),
     'L1_attn_bq': (0.0, 0.8),
     'L1_attn_bk': (0.0, 0.8),
     'L1_attn_bv': (0.0, 0.1),
     'L1_attn_bo': (0.0, 0.1)}
    factors = {'L0_ffn_gate_w': 3.898,
     'L0_ffn_w_gate': 2.885,
     'L0_ffn_w_up': 2.851,
     'L0_ffn_w_down': 2.853,
     'L1_attn_Wq': 8.0,
     'L1_attn_Wk': 8.0,
     'L1_attn_Wv': 4.342,
     'L1_ffn_gate_w': 8.0,
     'L1_ffn_wg': 8.0,
     'L1_ffn_wu': 8.0,
     'L1_ffn_wd': 8.0,
     'L1_ffn_sg': 3.927,
     'L1_ffn_su': 3.859,
     'L1_ffn_sd': 3.86}
    for name, (base, spread) in spreads.items():
        noise = np.random.default_rng([zlib.crc32(name.encode()), seed]).standard_normal(out[name].shape)
        drawn = base * np.exp(spread * noise) if base else spread * noise
        out[name] = jnp.asarray(drawn.astype(out[name].dtype))
    for name, factor in factors.items():
        out[name] = (out[name] * factor).astype(out[name].dtype)
    return out
```

```python
from contextlib import ExitStack

import numpy as np
import concourse.bass as bass
from concourse import mybir

F32 = mybir.dt.float32
F32R = mybir.dt.float32r
BF16 = mybir.dt.bfloat16
ALU = mybir.AluOpType
ACT = mybir.ActivationFunctionType
X_AXIS = mybir.AxisListType.X

P = 128
BATCH, SEQ, CH = 2, 1024, 256
TILES = SEQ // P
ALL_TILES = BATCH * TILES
KB = CH // P
BANK = 512
QCH = 512
EPS = 1e-5
MASKED = -1e30


class Engine:

    def __init__(self, sem, one_by_one=False):
        self.sem, self.count, self.queue = sem, 0, []
        self.one_by_one = one_by_one

    def __call__(self, issue, *waits):
        if self.one_by_one and self.count:
            waits += ((self.sem, self.count),)
        self.count += 1
        self.queue.append((issue, tuple(flat(waits)), True))
        return (self.sem, self.count)

    def quiet(self, issue, *waits):
        self.queue.append((issue, tuple(flat(waits)), False))

    def play(self, eng):
        reached = {}
        for issue, waits, signals in self.queue:
            for sem, value in waits:
                if reached.get(sem, 0) < value:
                    eng.wait_ge(sem, value)
                    reached[sem] = value
            inst = issue(eng)
            if signals:
                inst.then_inc(self.sem, 1)


def flat(waits):
    for w in waits:
        if w is None:
            continue
        if isinstance(w, list):
            yield from flat(w)
        else:
            yield w


class Ring:

    def __init__(self, n):
        self.readers, self.at = [None] * n, 0

    def take(self):
        slot = self.at
        self.at = (self.at + 1) % len(self.readers)
        return slot, self.readers[slot]

    def give(self, slot, *tokens):
        self.readers[slot] = list(tokens)


def copy_on_pool(eng, out, in_):
    return eng.tensor_scalar(out, in_, 1.0, 0.0, ALU.mult, ALU.add)


class AttentionShape:

    def __init__(self, heads, softmax):
        self.heads, self.softmax = heads, softmax
        self.d = CH // heads
        self.rows = 32 if softmax else 64
        self.heads_per_group = P // self.rows
        self.groups = heads // self.heads_per_group
        self.quads = heads // 4
        self.groups_per_quad = 4 // self.heads_per_group
        self.v_row = heads * (self.d + 1) + 32


def build_program(nc, ins, out):
    ctx = ExitStack()
    with ctx:
        def sb(name, shape, dt=F32, stack=ctx):
            return stack.enter_context(nc.sbuf_tensor(name, shape, dt))

        def sem(name):
            return ctx.enter_context(nc.semaphore(name))

        pe, act, dve = (Engine(sem(f"{n}_done")) for n in ("pe", "act", "dve"))
        pool = Engine(sem("pool_done"), one_by_one=True)
        sync = Engine(None)

        def load(name, dst, src, *waits):
            s = sem(f"loaded_{name}")
            sync.quiet(lambda e: e.dma_start(dst, src).then_inc(s, 16), *waits)
            return (s, 16)

        def fence():
            return [(e.sem, e.count) for e in (pe, act, dve, pool)]

        psum = ctx.enter_context(nc.psum_tensor("psum", [P, 8 * BANK], F32))
        pairs = Ring(3)
        o_banks = Ring(2)

        x = sb("x", [P, ALL_TILES, CH])
        stage = sb("stage", [P, 3072])
        ident = sb("ident", [P, P])
        ident_bf = sb("ident_bf", [P, P], BF16)
        later = sb("later", [P, 2, P])
        later_bf = sb("later_bf", [P, 2, P], BF16)
        ln_stats = sb("ln_stats", [P, ALL_TILES, 6])
        ln_mean_var = sb("ln_mean_var", [P, ALL_TILES, 2])
        ln_sd = sb("ln_sd", [P, ALL_TILES])
        ln_rstd = sb("ln_rstd", [P, ALL_TILES])

        x_dram = ins["x"].rearrange("b (t p) c -> p (b t) c", p=P)
        out_dram = out.rearrange("b (t p) c -> p (b t) c", p=P)
        ident_in = load("ident", ident[:], ins["ident"])
        x_ready = [None] * (ALL_TILES // 4)
        for c in range(ALL_TILES // 4):
            x_ready[c] = load(f"x{c}", x[:, 4 * c:4 * c + 4, :], x_dram[:, 4 * c:4 * c + 4, :])
        later_in = load("later", later[:], ins["later"])
        mask_ready = [dve(lambda e: e.tensor_copy(ident_bf[:], ident[:]), ident_in),
                      dve(lambda e: e.tensor_copy(later_bf[:], later[:]), later_in)]

        def split(src, hi, lo, src_ready, free=None):
            t = pool(lambda e: copy_on_pool(e, hi, src), src_ready, free)
            return pool(lambda e: e.tensor_tensor(lo, src, hi.bitcast(F32), ALU.subtract), t)

        def products(dst, lhs, rhs, last=True, first=True):
            terms = []
            for (lh, ll), (rh, rl) in zip(lhs, rhs):
                terms += [(lh, rh), (lh, rl), (ll, rh)]
            return [(lambda e, a=a, b=b, s=first and i == 0, z=last and i == len(terms) - 1:
                     e.matmul(dst, a, b, start=s, stop=z)) for i, (a, b) in enumerate(terms)]

        def to_channels(src, hi, lo, src_ready, free):
            slot, slot_free = pairs.take()
            bank = psum[:, slot * 1024:(slot + 1) * 1024].rearrange("p (k n) -> p k n", k=KB)
            for k in range(KB):
                for i in range(4):
                    t = (lambda e, k=k, i=i, tile=src(i): e.transpose(
                        bank[:, k, i * P:(i + 1) * P], tile[:, k * P:(k + 1) * P], ident[:]))
                    if (k, i) == (KB - 1, 3):
                        turned = pe(t)
                    else:
                        pe.quiet(t, src_ready, slot_free, ident_in)
            hi_done = act(lambda e: e.activation(hi, bank, ACT.Copy), turned, free)
            lo_done = dve(lambda e: e.tensor_tensor(lo, bank, hi.bitcast(F32), ALU.subtract),
                          hi_done, free)
            pairs.give(slot, lo_done)
            return [hi_done, lo_done]

        def layernorm(c, ready):
            t0, t1 = 4 * c, 4 * c + 4
            stats = [dve(lambda e, t=t: e.bn_stats(ln_stats[:, t, :], x[:, t, :]), ready)
                     for t in range(t0, t1)]
            for t in range(t0, t1):
                moments = dve(lambda e, t=t: e.bn_aggr(ln_mean_var[:, t, :], ln_stats[:, t, :]), stats[-1])
            sd = dve(lambda e: e.tensor_scalar(ln_sd[:, t0:t1], ln_mean_var[:, t0:t1, 1], EPS, None,
                                               ALU.add), moments)
            sd = act(lambda e: e.activation(ln_sd[:, t0:t1], ln_sd[:, t0:t1], ACT.Sqrt), sd)
            rstd = dve(lambda e: e.reciprocal(ln_rstd[:, t0:t1], ln_sd[:, t0:t1]), sd)
            done = [dve(lambda e, t=t: e.tensor_scalar(x[:, t, :], x[:, t, :], ln_mean_var[:, t, 0:1],
                                                       ln_rstd[:, t:t + 1], ALU.subtract, ALU.mult), rstd)
                    for t in range(t0, t1)]
            return done[-1]

        stage_free = [None]

        def attention(layer, shape, start):
            s = ExitStack()
            H, d, R = shape.heads, shape.d, shape.rows
            HG = shape.heads_per_group

            def buf(name, sh, dt=F32):
                return sb(f"{name}{layer}", sh, dt, s)

            w_hi = buf("wqkv_hi", [P, KB, 3 * CH], F32R)
            w_lo = buf("wqkv_lo", [P, KB, 3 * CH], F32R)
            wo_hi = buf("wo_hi", [P, KB, CH], F32R)
            wo_lo = buf("wo_lo", [P, KB, CH], F32R)
            cos = buf("cos", [P, TILES, 2, d])
            sin = buf("sin", [P, TILES, 2, d])
            qk = buf("qk", [P, TILES, 2, CH])
            v = buf("v", [P, TILES, shape.v_row])
            xt = buf("xt", [P, 2 * KB * SEQ], F32R)
            xt_hi = xt[:, 0:KB * SEQ].rearrange("p (k n) -> p k n", k=KB)
            xt_lo = xt[:, KB * SEQ:].rearrange("p (k n) -> p k n", k=KB)
            q_rows = buf("q_rows", [P, 2, TILES * P], F32R)
            k_rows = buf("k_rows", [P, 2, TILES * P], F32R)
            qt = buf("qt", [P, 4, SEQ], F32R)
            kt = buf("kt", [P, 2, SEQ])
            km = buf("km", [P, 2, 4, SEQ], F32R)
            probs = buf("probs", [P, 3, 4, QCH])
            o_cols = buf("o_cols", [P, 2, SEQ])
            ao = buf("ao", [P, TILES, CH])
            o_rcp = buf("o_rcp", [P, 2, TILES, 4])

            def masked_k(slot):
                return km[:, slot] if slot < 2 else xt[:, :].rearrange("p (h n) -> p h n", h=4)

            def pieces(rows, slot):
                return rows[:, slot, :].rearrange("p (t h f) -> p t h f", t=TILES, h=HG)

            w_in = load(f"wqkv{layer}", stage[:, 0:KB * 3 * CH].rearrange("p (k n) -> p k n", k=KB),
                        ins[f"wqkv{layer}"].rearrange("(k p) n -> p k n", p=P), stage_free[0])
            wo_in = load(f"wo{layer}", stage[:, KB * 3 * CH:KB * 4 * CH].rearrange("p (k n) -> p k n", k=KB),
                         ins[f"wo{layer}"].rearrange("(k p) n -> p k n", p=P), stage_free[0])
            cos_in = load(f"cos{layer}", cos[:], ins[f"cos{layer}"], start)
            sin_in = load(f"sin{layer}", sin[:], ins[f"sin{layer}"], start)
            w_ready = split(stage[:, 0:KB * 3 * CH], w_hi[:, :, :].rearrange("p k n -> p (k n)"),
                            w_lo[:, :, :].rearrange("p k n -> p (k n)"), w_in, start)
            wo_ready = split(stage[:, KB * 3 * CH:KB * 4 * CH], wo_hi[:, :, :].rearrange("p k n -> p (k n)"),
                             wo_lo[:, :, :].rearrange("p k n -> p (k n)"), wo_in, start)
            stage_free[0] = wo_ready
            v_ones = pool(lambda e: e.memset(v[:], 1.0), start)
            rows_clear = [dve(lambda e: e.memset(q_rows[:].bitcast(F32), 0.0), start),
                          dve(lambda e: e.memset(k_rows[:].bitcast(F32), 0.0), start),
                          dve(lambda e: e.memset(km[:].bitcast(F32), 0.0), start)]
            if shape.softmax:
                for slot in range(2):
                    rows_clear.append(dve(lambda e, slot=slot: e.memset(
                        pieces(k_rows, slot)[:, :, :, 3 * d:3 * d + 2].bitcast(F32), 1.0), rows_clear[1]))
                neg_max = buf("neg_max", [P, 2, TILES, 4])
                flat_ao = ao[0:2].rearrange("p t n -> p (t n)")
                bias, bias_low = flat_ao[:, 0:4 * CH], flat_ao[:, 4 * CH:8 * CH]
                bias_rows = buf("bias_rows", [2, 4 * CH], F32R)
                pick = buf("pick", [2, 2])
                ones_f = buf("ones_f", [2, P])
                ones = buf("ones", [2, P], F32R)
                b_in = [load(f"bias{r}", bias[r:r + 1, :], ins["bias"].rearrange("(a n) -> a n", a=1), start)
                        for r in range(2)]
                b_in.append(load("pick", pick[:], ins["pick"], start))
                b = dve(lambda e: e.tensor_copy(bias_rows[:], bias), b_in)
                b = dve(lambda e: e.tensor_tensor(bias_low, bias, bias_rows[:].bitcast(F32), ALU.subtract), b)
                b = dve(lambda e: e.tensor_scalar(bias_low, bias_low, pick[:, 1:2], None, ALU.mult), b)
                b = dve(lambda e: e.scalar_tensor_tensor(bias_rows[:], bias_rows[:].bitcast(F32), pick[:, 0:1],
                                                         bias_low, ALU.mult, ALU.add), b)
                o = dve(lambda e: e.memset(ones_f[:], 1.0), start)
                bias_ready = [b, dve(lambda e: e.tensor_copy(ones[:], ones_f[:]), o)]
            else:
                qk_scale = buf("qk_scale", [P, d])
                qk_bias = buf("qk_bias", [P, d])
                scale_in = load("qk_scale", qk_scale[:], ins["ln_scale"].partition_broadcast(P), start)
                shift_in = load("qk_bias", qk_bias[:], ins["ln_bias"].partition_broadcast(P), start)
                mom = buf("mom", [P, 3, 4, 2 * H])
                bias_ready = None

            q_taken = Ring(2)
            kt_taken = Ring(2)
            qt_taken = Ring(4) if not shape.softmax else (Ring(2), Ring(2))
            km_taken = Ring(3 if shape.softmax else 2)
            p_taken = Ring(3)
            oc_taken = Ring(2)

            for b in range(BATCH):
                before = fence() if b else start
                seq_x = x_ready[2 * b:2 * b + 2]

                xt_done = [to_channels(lambda i, c=c: x[:, b * TILES + 4 * c + i, :],
                                       xt_hi[:, :, c * 512:(c + 1) * 512], xt_lo[:, :, c * 512:(c + 1) * 512],
                                       seq_x[c], before) for c in range(2)]
                v_done, qk_done = [], [None] * TILES
                chain = {}

                def project(t):
                    slot, slot_free = pairs.take()
                    base = slot * 1024
                    cols = slice(t * P, (t + 1) * P)
                    first = True
                    for k in range(KB):
                        for a, w in ((xt_hi, w_hi), (xt_hi, w_lo), (xt_lo, w_hi)):
                            end = k == KB - 1 and a is xt_lo and not shape.softmax
                            pe.quiet(lambda e, a=a, w=w, k=k, f=first, z=end: e.matmul(
                                psum[:, base:base + 512], a[:, k, cols], w[:, k, 0:512], start=f, stop=z),
                                xt_done[t // 4], slot_free, w_ready)
                            mm = (lambda e, a=a, w=w, k=k, f=first, z=end: e.matmul(
                                psum[:, base + 512:base + 768], a[:, k, cols], w[:, k, 512:768], start=f, stop=z))
                            first = False
                            if end:
                                projected = pe(mm)
                            else:
                                pe.quiet(mm)
                    if shape.softmax:
                        pe.quiet(lambda e: e.matmul(psum[:, base:base + 512], ones[:], bias_rows[:, 0:512],
                                                    start=False, stop=True), bias_ready)
                        projected = pe(lambda e: e.matmul(psum[:, base + 512:base + 768], ones[:],
                                                          bias_rows[:, 512:768], start=False, stop=True))
                    vv = v[:, t, 0:H * (d + 1)].rearrange("p (h e) -> p h e", h=H)[:, :, 0:d]
                    v_out = act(lambda e: e.activation(
                        vv, psum[:, base + 512:base + 768].rearrange("p (h e) -> p h e", h=H), ACT.Copy),
                        projected, v_ones, before)
                    v_done.append(v_out)

                    u = t % 3
                    pq = psum[:, base:base + 512].rearrange("p (s h e) -> p s h e", s=2, h=H)
                    ra = probs[:, u, 0, :].rearrange("p (s h e) -> p s h e", s=2, h=H)
                    rb = probs[:, u, 1, :].rearrange("p (s h e) -> p s h e", s=2, h=H)
                    h2 = d // 2

                    def table(tb, lo, hi):
                        return tb[:, t, :, lo:hi].unsqueeze(2).to_broadcast([P, 2, H, hi - lo])

                    free = [before, chain.get(("free", u))]
                    a1 = dve(lambda e: e.tensor_tensor(ra, pq, table(cos, 0, d), ALU.mult),
                             projected, cos_in, free)
                    dve(lambda e: e.tensor_tensor(rb[:, :, :, 0:h2], pq[:, :, :, h2:d], table(sin, 0, h2),
                                                  ALU.mult), sin_in)
                    b2 = dve(lambda e: e.tensor_tensor(rb[:, :, :, h2:d], pq[:, :, :, 0:h2],
                                                       table(sin, h2, d), ALU.mult))
                    pairs.give(slot, v_out, b2)
                    if shape.softmax:
                        done = dve(lambda e: e.tensor_tensor(qk[:, t].rearrange("p s (h e) -> p s h e", h=H),
                                                             ra, rb, ALU.add), b2)
                        qk_done[t] = done
                        chain["free", u] = done
                        return
                    ra2 = probs[:, u, 0, :].rearrange("p (g e) -> p g e", e=d)
                    rb2 = probs[:, u, 1, :].rearrange("p (g e) -> p g e", e=d)
                    m = mom[:, u]
                    r = dve(lambda e: e.tensor_tensor(probs[:, u, 0, :], probs[:, u, 0, :], probs[:, u, 1, :],
                                                      ALU.add), b2)
                    r = dve(lambda e: e.tensor_reduce(m[:, 0], ra2, X_AXIS, ALU.add), r)
                    r = dve(lambda e: e.tensor_scalar(m[:, 0], m[:, 0], 1.0 / d, None, ALU.mult), r)
                    r = dve(lambda e: e.tensor_tensor(ra2, ra2, m[:, 0].unsqueeze(2).to_broadcast([P, 2 * H, d]),
                                                      ALU.subtract), r)
                    chain["sq", t] = act(lambda e: e.activation(rb2, ra2, ACT.Square), r)

                def spread(t):
                    u = t % 3
                    m = mom[:, u]
                    rb2 = probs[:, u, 1, :].rearrange("p (g e) -> p g e", e=d)
                    r = dve(lambda e: e.tensor_reduce(m[:, 1], rb2, X_AXIS, ALU.add), chain["sq", t])
                    r = dve(lambda e: e.tensor_scalar(m[:, 1], m[:, 1], 1.0 / d, EPS, ALU.mult, ALU.add), r)
                    chain["sd", t] = act(lambda e: e.activation(m[:, 2], m[:, 1], ACT.Sqrt), r)

                def scale(t):
                    u = t % 3
                    m = mom[:, u]
                    ra2 = probs[:, u, 0, :].rearrange("p (g e) -> p g e", e=d)
                    r = dve(lambda e: e.reciprocal(m[:, 3], m[:, 2]), chain["sd", t])
                    r = pool(lambda e: e.tensor_tensor(ra2, ra2, m[:, 3].unsqueeze(2).to_broadcast([P, 2 * H, d]),
                                                       ALU.mult), r)
                    r = pool(lambda e: e.tensor_tensor(ra2, ra2, qk_scale[:].unsqueeze(1).to_broadcast([P, 2 * H, d]),
                                                       ALU.mult), r, scale_in)
                    done = pool(lambda e: e.tensor_tensor(
                        qk[:, t].rearrange("p s (h e) -> p (s h) e", h=H), ra2,
                        qk_bias[:].unsqueeze(1).to_broadcast([P, 2 * H, d]), ALU.add), r, shift_in, before)
                    qk_done[t] = done
                    chain["free", u] = done

                for t in range(TILES + 2):
                    if t < TILES:
                        project(t)
                    if not shape.softmax:
                        if 1 <= t <= TILES:
                            spread(t - 1)
                        if 2 <= t:
                            scale(t - 2)
                projected_all = (pe.sem, pe.count)
                if shape.softmax:
                    rows_clear.append(dve(lambda e: e.memset(xt[:].bitcast(F32), 0.0), projected_all))
                    km_taken.give(2, rows_clear[-1])

                group_ready, qt_ready, km_ready = {}, {}, {}

                def prepare(g):
                    slot, free = q_taken.take()
                    hd = slice(g * HG * d, (g + 1) * HG * d)

                    def src(which):
                        return qk[:, :, which, hd].rearrange("p t (h e) -> p t h e", h=HG)

                    def put(rows, at):
                        return pieces(rows, slot)[:, :, :, at * d:(at + 1) * d]

                    hi_at = ((0, 1), (0, 2))
                    lo_at = ((2,), (1,)) if shape.softmax else ((2, 3), (1, 3))
                    waits = [qk_done, rows_clear, free]
                    done = []
                    for which, rows in ((0, q_rows), (1, k_rows)):
                        h = pool(lambda e, w=which, r=rows: copy_on_pool(
                            e, put(r, hi_at[w][0]), src(w)), waits)
                        pool(lambda e, w=which, r=rows: copy_on_pool(e, put(r, hi_at[w][1]), src(w)))
                        low = pool(lambda e, w=which, r=rows: e.tensor_tensor(
                            put(r, lo_at[w][0]), src(w), put(r, hi_at[w][0]).bitcast(F32), ALU.subtract), h)
                        if not shape.softmax:
                            low = pool(lambda e, w=which, r=rows: copy_on_pool(
                                e, put(r, 3), put(r, lo_at[w][0]).bitcast(F32)), low)
                        elif which == 0:
                            low = pool(lambda e: e.memset(
                                pieces(q_rows, slot)[:, :, :, 3 * d:3 * d + 2].bitcast(F32), 0.0))
                        done.append(low)
                    group_ready[g] = slot

                    def turn(rows, ready):
                        pair, pair_free = pairs.take()
                        for t in range(TILES):
                            tr = (lambda e, t=t: e.transpose(
                                psum[:, pair * 1024 + t * P:pair * 1024 + (t + 1) * P],
                                rows[:, slot, t * P:(t + 1) * P].bitcast(F32), ident[:]))
                            if t == TILES - 1:
                                turned = pe(tr)
                            else:
                                pe.quiet(tr, ready, pair_free)
                        return pair, turned

                    ring = qt_taken[0] if shape.softmax else qt_taken
                    q_slot, q_free = ring.take()
                    pair, turned = turn(q_rows, done[0])
                    q_out = act(lambda e, pair=pair: e.activation(
                        qt[:, q_slot, :], psum[:, pair * 1024:(pair + 1) * 1024], ACT.Copy), turned, q_free, before)
                    pairs.give(pair, q_out)
                    qt_ready[g] = (q_slot, q_out)
                    k_slot, k_free = kt_taken.take()
                    pair, turned = turn(k_rows, done[1])
                    if not shape.softmax:
                        q_taken.give(slot, turned)
                    k_out = act(lambda e: e.activation(kt[:, k_slot, :], psum[:, pair * 1024:(pair + 1) * 1024],
                                                       ACT.Copy), turned, k_free, before)
                    pairs.give(pair, k_out)
                    quad, part = divmod(g, shape.groups_per_quad)
                    if part == 0:
                        m_slot, m_free = km_taken.take()
                        km_ready[quad] = [m_slot, m_free]
                    m_slot, m_free = km_ready[quad][0:2]
                    for h in range(HG):
                        r = slice(h * R, (h + 1) * R)
                        m_out = pool(lambda e, h=h, r=r: copy_on_pool(
                            e, masked_k(m_slot)[r, part * HG + h, :], kt[r, k_slot, :]), k_out, m_free, rows_clear)
                    km_ready[quad].append(m_out)
                    kt_taken.give(k_slot, m_out)

                max_done = {}

                def max_units(g):
                    units = []
                    for i in range(TILES):
                        w = (i + 1) * P
                        per = 4 if w <= 256 else 2 if w <= 512 else 1
                        for h0 in range(0, 4, per):
                            units.append((i, w, h0, per))
                    return units

                def max_unit(g, unit):
                    i, w, h0, n = unit
                    slot, slot_free = pairs.take()
                    base = slot * 1024
                    stride = w if n > 1 and w <= 256 else 512 if n > 1 else 1024
                    q_slot, q_ready = qt_ready[g]
                    keys = masked_k(km_ready[g][0])
                    for h in range(h0, h0 + n):
                        at = base + (h - h0) * stride
                        for c0 in range(0, w, 512):
                            cw = min(512, w - c0)
                            diagonal = c0 + cw == w
                            pe.quiet(lambda e, h=h, at=at, c0=c0, cw=cw, z=not diagonal: e.matmul(
                                psum[:, at + c0:at + c0 + cw], qt[:, q_slot, i * P:(i + 1) * P],
                                keys[:, h, c0:c0 + cw], start=True, stop=z),
                                slot_free, q_ready, km_ready[g][2:], mask_ready)
                            if diagonal:
                                mm = (lambda e, at=at: e.matmul(psum[:, at + w - P:at + w], ident_bf[:],
                                                                later_bf[:, 0, :], start=False, stop=True))
                                if h == h0 + n - 1:
                                    scored = pe(mm)
                                else:
                                    pe.quiet(mm)
                    view = psum[:, base:base + n * stride].rearrange("p (h n) -> p h n", h=n)[:, :, 0:w]
                    m = dve(lambda e: e.tensor_reduce(neg_max[:, g % 2, i, h0:h0 + n], view, X_AXIS, ALU.max,
                                                      negate=True), scored, max_done.get(("read", g - 2)), before)
                    pairs.give(slot, m)
                    max_done[g, i] = m
                    if i == TILES - 1 and h0 == 3:
                        qt_taken[0].give(q_slot, scored)

                def place_max(g, half):
                    slot = group_ready[g]
                    t0, t1 = half * 4, half * 4 + 4
                    nm = neg_max[:, g % 2, t0:t1, :].unsqueeze(3)
                    at = pieces(q_rows, slot)[:, t0:t1, :, 3 * d:3 * d + 1]
                    at_lo = pieces(q_rows, slot)[:, t0:t1, :, 3 * d + 1:3 * d + 2]
                    m = pool(lambda e: copy_on_pool(e, at, nm), max_done[g, t1 - 1])
                    m = pool(lambda e: e.tensor_tensor(at_lo, nm, at.bitcast(F32), ALU.subtract), m)
                    if half:
                        max_done["read", g] = m
                    pair, pair_free = pairs.take()
                    for t in range(t0, t1):
                        tr = (lambda e, t=t: e.transpose(
                            psum[:, pair * 1024 + (t - t0) * P:pair * 1024 + (t - t0 + 1) * P],
                            q_rows[:, slot, t * P:(t + 1) * P].bitcast(F32), ident[:]))
                        if t == t1 - 1:
                            turned = pe(tr)
                        else:
                            pe.quiet(tr, m, pair_free)
                    if half:
                        q_taken.give(slot, turned)
                    if half == 0:
                        q_slot, q_free = qt_taken[1].take()
                        qt_ready["max", g] = [q_slot, q_free]
                    q_slot, q_free = qt_ready["max", g][0:2]
                    q_out = act(lambda e: e.activation(qt[:, 2 + q_slot, half * 512:(half + 1) * 512],
                                                       psum[:, pair * 1024:pair * 1024 + 512], ACT.Copy),
                                turned, q_free, before)
                    pairs.give(pair, q_out)
                    qt_ready["max", g].append(q_out)

                weighed = []
                o_turn = {}

                def weigh(step):
                    quad, c, key, q0, w, slot, ready, bank, bank_free = step
                    for h in range(4):
                        at = (4 * quad + h) * (d + 1)
                        mm = (lambda e, h=h, at=at: e.matmul(
                            psum[32 * h:32 * h + 32, bank + q0:bank + QCH], v[:, key, at:at + 32],
                            probs[:, slot, h, 0:w], start=(key == 0), stop=(key == 4 * c + 3)))
                        if h == 3:
                            done = pe(mm)
                        else:
                            pe.quiet(mm, ready, bank_free, v_done)
                    p_taken.give(slot, done)
                    if key == 4 * c + 3:
                        if c == 0:
                            o_turn[quad] = list(oc_taken.take())
                        oc, oc_free = o_turn[quad][0:2]
                        o_out = act(lambda e: e.activation(o_cols[:, oc, c * QCH:(c + 1) * QCH],
                                                           psum[:, bank:bank + QCH], ACT.Copy), done, oc_free)
                        o_turn[quad].append(o_out)
                        o_banks.give((bank - 6 * BANK) // BANK, o_out)

                def weights_step(quad, c, key, bank, bank_free):
                    j = key - 4 * c
                    q0 = max(j, 0) * P
                    w = QCH - q0
                    per = 2 if w > 256 else 4
                    keys = masked_k(km_ready[quad][0])
                    masks = j >= 0 and shape.softmax
                    p_slot, p_free = p_taken.take()
                    ready = []
                    for h0 in range(0, 4, per):
                        slot, slot_free = pairs.take()
                        base = slot * 1024
                        stride = 512 if per == 2 else w
                        for h in range(h0, h0 + per):
                            if shape.softmax:
                                q_slot, q_ready = 2 + qt_ready["max", quad][0], qt_ready["max", quad][2 + c]
                            else:
                                q_slot, q_ready = qt_ready[2 * quad + h // 2]
                            at = base + (h - h0) * stride
                            mm = (lambda e, h=h, at=at, q_slot=q_slot: e.matmul(
                                psum[:, at:at + w], keys[:, h, key * P:(key + 1) * P],
                                qt[:, q_slot, c * QCH + q0:(c + 1) * QCH], start=True, stop=not masks))
                            if masks:
                                pe.quiet(mm, slot_free, q_ready, km_ready[quad][2:])
                                mm = (lambda e, at=at: e.matmul(psum[:, at:at + P], ident_bf[:], later_bf[:, 1, :],
                                                                start=False, stop=True))
                            if h == h0 + per - 1:
                                scored = pe(mm, q_ready)
                            else:
                                pe.quiet(mm, slot_free, q_ready, km_ready[quad][2:])
                        view = psum[:, base:base + per * stride].rearrange("p (h n) -> p h n", h=per)[:, :, 0:w]
                        dst = probs[:, p_slot, h0:h0 + per, 0:w]
                        t = act(lambda e, view=view, dst=dst: e.activation(
                            dst, view, ACT.Exp if shape.softmax else ACT.Square), scored, p_free, qk_done)
                        pairs.give(slot, t)
                        if not shape.softmax:
                            where = pool if (key + h0 // 2) % 4 == 3 and j < 0 else dve
                            t = where(lambda e, dst=dst: e.tensor_tensor(dst, dst, dst, ALU.mult), t)
                        ready.append(t)
                    if j >= 0 and not shape.softmax:
                        dst = probs[:, p_slot, :, 0:P]
                        ready.append(pool(lambda e: e.affine_select(
                            out=dst, in_=dst, compare_op=ALU.is_ge, fill=0.0, base=0,
                            pattern=[[0, 4], [1, P]], channel_multiplier=-1), ready[:]))
                    if key == 4 * c + 3 and c == 1:
                        km_taken.give(km_ready[quad][0], scored)
                        if shape.softmax:
                            qt_taken[1].give(qt_ready["max", quad][0], scored)
                        else:
                            for g in (2 * quad, 2 * quad + 1):
                                qt_taken.give(qt_ready[g][0], scored)
                    while weighed:
                        weigh(weighed.pop())
                    weighed.append((quad, c, key, q0, w, p_slot, ready, bank, bank_free))

                def normalize(quad):
                    while weighed and weighed[0][0] == quad:
                        weigh(weighed.pop())
                    oc = o_turn[quad][0]
                    pair, pair_free = pairs.take()
                    for t in range(TILES):
                        tr = (lambda e, t=t: e.transpose(
                            psum[:, pair * 1024 + t * P:pair * 1024 + (t + 1) * P],
                            o_cols[:, oc, t * P:(t + 1) * P], ident[:]))
                        if t == TILES - 1:
                            turned = pe(tr)
                        else:
                            pe.quiet(tr, o_turn[quad][2:], pair_free)
                    oc_taken.give(oc, turned)
                    o = psum[:, pair * 1024:(pair + 1) * 1024].rearrange("p (t h e) -> p t h e", t=TILES, h=4)
                    r = dve(lambda e: e.reciprocal(o_rcp[:, quad % 2].unsqueeze(3), o[:, :, :, d:d + 1]), turned,
                            before)
                    dst = ao[:, :, quad * 4 * d:(quad + 1) * 4 * d].rearrange("p t (h e) -> p t h e", h=4)
                    done = dve(lambda e: e.tensor_tensor(
                        dst, o[:, :, :, 0:d], o_rcp[:, quad % 2].unsqueeze(3).to_broadcast([P, TILES, 4, d]),
                        ALU.mult), r)
                    pairs.give(pair, done)
                    return done

                if shape.softmax:
                    prepare(0)
                    prepare(1)
                    for unit in max_units(0):
                        max_unit(0, unit)
                    place_max(0, 0)
                else:
                    prepare(0)
                    prepare(1)
                for quad in range(shape.quads):
                    steps = []
                    for c in range(SEQ // QCH):
                        bank, bank_free = o_banks.take()
                        steps += [(c, key, 6 * BANK + bank * BANK, bank_free) for key in range(4 * c + 4)]
                        o_banks.give(bank, None)
                    between = []
                    if quad:
                        between.append((3, lambda q=quad - 1: normalize(q)))
                    if shape.softmax:
                        between.append((2, lambda q=quad: place_max(q, 1)))
                        if quad + 2 < shape.quads:
                            between.append((6, lambda q=quad + 2: prepare(q)))
                        if quad + 1 < shape.quads:
                            units = max_units(quad + 1)
                            for n, unit in enumerate(units):
                                between.append((1 + n * 11 / len(units),
                                                lambda q=quad + 1, unit=unit: max_unit(q, unit)))
                            between.append((12, lambda q=quad + 1: place_max(q, 0)))
                    elif quad + 1 < shape.quads:
                        between.append((5, lambda q=quad: prepare(2 * q + 2)))
                        between.append((9, lambda q=quad: prepare(2 * q + 3)))
                    between.sort(key=lambda p: p[0])
                    for n, (c, key, bank, bank_free) in enumerate(steps):
                        while between and between[0][0] <= n:
                            between.pop(0)[1]()
                        weights_step(quad, c, key, bank, o_free(o_banks, bank) if key == 0 else None)
                    for _, what in between:
                        what()
                ao_done = normalize(shape.quads - 1)

                for c in range(2):
                    cols = slice(c * 512, (c + 1) * 512)
                    turned = to_channels(lambda i, c=c: ao[:, 4 * c + i, :], xt_hi[:, :, cols], xt_lo[:, :, cols],
                                         ao_done, (pe.sem, pe.count))
                    slot, slot_free = pairs.take()
                    base = slot * 1024
                    for i in range(4):
                        dst = psum[:, base + i * CH:base + (i + 1) * CH]
                        tk = slice((4 * c + i) * P, (4 * c + i + 1) * P)
                        todo = products(dst, [(xt_hi[:, k, tk], xt_lo[:, k, tk]) for k in range(KB)],
                                        [(wo_hi[:, k, :], wo_lo[:, k, :]) for k in range(KB)],
                                        last=not shape.softmax)
                        if shape.softmax:
                            todo.append(lambda e, dst=dst: e.matmul(dst, ones[:], bias_rows[:, 3 * CH:4 * CH],
                                                                    start=False, stop=True))
                        for mm in todo[:-1]:
                            pe.quiet(mm, turned, slot_free, wo_ready)
                        projected = pe(todo[-1])
                    g = 2 * b + c
                    xs = x[:, 4 * g:4 * g + 4, :].rearrange("p t n -> p (t n)")
                    added = dve(lambda e, base=base, xs=xs: e.tensor_tensor(xs, psum[:, base:base + 1024], xs, ALU.add),
                                projected, x_ready[g])
                    pairs.give(slot, added)
                    x_ready[g] = layernorm(g, added)
            s.close()

        def o_free(ring, bank):
            return ring.readers[(bank - 6 * BANK) // BANK]

        w_loads = [sem("loaded_weights"), 0]

        def experts(layer, start, groups, n_experts):
            s = ExitStack()

            def buf(name, sh, dt=F32):
                return sb(f"{name}{layer}", sh, dt, s)

            T = BATCH * SEQ
            xt_hi = buf("fxt_hi", [P, KB, T], F32R)
            xt_lo = buf("fxt_lo", [P, KB, T], F32R)
            parts = {n: (buf(f"{n}_hi", [P, 2, 1024], F32R), buf(f"{n}_lo", [P, 2, 1024], F32R))
                     for n in ("gate", "up", "down")}
            silu = buf("silu", [P, 2, 512])
            hid = buf("hid", [P, 2, 512])
            hid_hi = buf("hid_hi", [P, 2, 512], F32R)
            hid_lo = buf("hid_lo", [P, 2, 512], F32R)
            gw = buf("gw", [P, KB, n_experts])
            gw_hi = buf("gw_hi", [P, KB, n_experts], F32R)
            gw_lo = buf("gw_lo", [P, KB, n_experts], F32R)
            E = n_experts

            gw_in = load(f"gw{layer}", gw[:], ins[f"router{layer}"].rearrange("(k p) n -> p k n", p=P), start)
            gw_ready = split(gw[:], gw_hi[:], gw_lo[:], gw_in, start)

            w_free = Ring(2)
            w_state = {}

            def weight_work(n):
                f0, width, tiles, _ = groups[n]
                cols = width * tiles
                box = {}

                def bring():
                    slot, free = w_free.take()
                    box["slot"], box["free"] = slot, free
                    srcs = {
                        "gate": (stage[:, 0:KB * cols].rearrange("p (k n) -> p k n", k=KB),
                                 ins[f"gate{layer}"][:, f0:f0 + cols].rearrange("(k p) n -> p k n", p=P)),
                        "up": (stage[:, 1024:1024 + KB * cols].rearrange("p (k n) -> p k n", k=KB),
                               ins[f"up{layer}"][:, f0:f0 + cols].rearrange("(k p) n -> p k n", p=P)),
                        "down": (stage[0:width, 2048:2048 + tiles * CH].rearrange("p (k n) -> p k n", k=tiles),
                                 ins[f"down{layer}"][f0:f0 + cols, :].rearrange("(k p) n -> p k n", p=width)),
                    }
                    for dst, src in srcs.values():
                        w_loads[1] += 16
                        sync.quiet(lambda e, dst=dst, src=src: e.dma_start(dst, src).then_inc(w_loads[0], 16),
                                   stage_free[0])
                    box["in"] = (w_loads[0], w_loads[1])

                work = [bring]
                for i, name in enumerate(("gate", "up", "down")):
                    rows = width if name == "down" else P
                    n_cols = tiles * CH if name == "down" else KB * cols

                    def cut(which, i=i, name=name, rows=rows, n_cols=n_cols):
                        src = stage[0:rows, i * 1024:i * 1024 + n_cols]
                        hi, lo = (p[0:rows, box["slot"], 0:n_cols] for p in parts[name])
                        if which == 0:
                            box["t"] = pool(lambda e: copy_on_pool(e, hi, src), box["in"], box["free"], start)
                        else:
                            box["t"] = pool(lambda e: e.tensor_tensor(lo, src, hi.bitcast(F32), ALU.subtract),
                                            box["t"])
                            if name == "down":
                                stage_free[0] = box["t"]
                                w_state[n] = (box["slot"], box["t"])

                    work += [lambda c=cut: c(0), lambda c=cut: c(1)]
                return work

            for w in weight_work(0):
                w()

            logits = buf("logits", [P, ALL_TILES, E])
            xt_done = []
            lg_slot, lg_free = pairs.take()
            lg_base = lg_slot * 1024
            for c in range(4):
                cols = slice(c * 512, (c + 1) * 512)
                if pairs.at == lg_slot:
                    pairs.take()
                xt_done.append(to_channels(lambda i, c=c: x[:, 4 * c + i, :], xt_hi[:, :, cols],
                                           xt_lo[:, :, cols], x_ready[c], start))
                for t in range(4 * c, 4 * c + 4):
                    tk = slice(t * P, (t + 1) * P)
                    todo = products(psum[:, lg_base + t * E:lg_base + (t + 1) * E],
                                    [(xt_hi[:, k, tk], xt_lo[:, k, tk]) for k in range(KB)],
                                    [(gw_hi[:, k, :], gw_lo[:, k, :]) for k in range(KB)])
                    for mm in todo[:-1]:
                        pe.quiet(mm, xt_done[c], lg_free, gw_ready)
                    lg = pe(todo[-1])
            lg_out = dve(lambda e: e.tensor_copy(logits[:], psum[:, lg_base:lg_base + ALL_TILES * E].rearrange(
                "p (t n) -> p t n", n=E)), lg, start)
            pairs.give(lg_slot, lg_out)

            if E == 2:
                top = buf("top", [P, ALL_TILES])
                prob = buf("prob", [P, ALL_TILES, E])
                tot = buf("tot", [P, ALL_TILES])
                is_top = buf("is_top", [P, ALL_TILES, E])
                coef = buf("coef", [P, ALL_TILES, E])
                l0, l1 = logits[:, :, 0], logits[:, :, 1]
                r = dve(lambda e: e.tensor_tensor(top[:], l0, l1, ALU.max), lg_out)
                r = dve(lambda e: e.tensor_tensor(prob[:], logits[:], top[:].unsqueeze(2).to_broadcast(
                    [P, ALL_TILES, E]), ALU.subtract), r)
                r = act(lambda e: e.activation(prob[:], prob[:], ACT.Exp), r)
                r = dve(lambda e: e.tensor_tensor(tot[:], prob[:, :, 0], prob[:, :, 1], ALU.add), r)
                r = dve(lambda e: e.reciprocal(tot[:], tot[:]), r)
                r = dve(lambda e: e.tensor_tensor(prob[:], prob[:], tot[:].unsqueeze(2).to_broadcast(
                    [P, ALL_TILES, E]), ALU.mult), r)
                dve(lambda e: e.tensor_tensor(is_top[:, :, 0], prob[:, :, 0], prob[:, :, 1], ALU.is_ge), r)
                r = dve(lambda e: e.tensor_tensor(is_top[:, :, 1], prob[:, :, 1], prob[:, :, 0], ALU.is_gt), r)
                coef_ready = dve(lambda e: e.tensor_tensor(coef[:], prob[:], is_top[:], ALU.mult), r)
            else:
                TOP_K = 6
                score = buf("score", [P, ALL_TILES, E + 8 - TOP_K])
                best = buf("best", [P, ALL_TILES, 8])
                rest = buf("rest", [P, ALL_TILES, E + 8 - TOP_K])
                tot = buf("tot", [P, ALL_TILES])
                comb = buf("comb", [P, ALL_TILES, E])
                comb_rows = buf("comb_rows", [P, ALL_TILES, P], F32R)
                comb_t = buf("comb_t", [P, T], F32R)
                F = groups[-1][0]
                pick_f = buf("pick_f", [P, F], F32R)
                sc = score[:, :, 0:E]
                dve(lambda e: e.memset(score[:], -1.0), start)
                cleared = dve(lambda e: e.memset(comb_rows[:].bitcast(F32), 0.0), start)
                r = act(lambda e: e.activation(logits[:], logits[:], ACT.Exp, scale=-1.0), lg_out)
                r = dve(lambda e: e.tensor_scalar(logits[:], logits[:], 1.0, None, ALU.add), r)
                r = dve(lambda e: e.reciprocal(sc, logits[:]), r)
                for t in range(ALL_TILES):
                    b8 = dve(lambda e, t=t: e.max(best[:, t, :], score[:, t, 0:E]), r)
                low = dve(lambda e: e.memset(best[:, :, TOP_K:8], -1.0), b8)
                for t in range(ALL_TILES):
                    mr = dve(lambda e, t=t: e.match_replace(rest[:, t, :], best[:, t, :], score[:, t, :], -2.0), low)
                r = dve(lambda e: e.tensor_tensor(comb[:], rest[:, :, 0:E], sc, ALU.not_equal), mr)
                r = dve(lambda e: e.tensor_tensor(comb[:], comb[:], sc, ALU.mult), r)
                r = dve(lambda e: e.tensor_reduce(tot[:], comb[:], X_AXIS, ALU.add), r)
                r = dve(lambda e: e.tensor_scalar(tot[:], tot[:], 1e-20, None, ALU.add), r)
                r = dve(lambda e: e.reciprocal(tot[:], tot[:]), r)
                r = dve(lambda e: e.tensor_tensor(comb[:], comb[:], tot[:].unsqueeze(2).to_broadcast(
                    [P, ALL_TILES, E]), ALU.mult), r)
                r = dve(lambda e: e.tensor_copy(comb_rows[:, :, 0:E], comb[:]), r, cleared)
                r = dve(lambda e: e.tensor_tensor(comb_rows[:, :, E:2 * E], comb[:],
                                                  comb_rows[:, :, 0:E].bitcast(F32), ALU.subtract), r)
                comb_done = []
                for c in range(2):
                    slot, slot_free = pairs.take()
                    for i in range(8):
                        tr = (lambda e, i=i, c=c, slot=slot: e.transpose(
                            psum[:, slot * 1024 + i * P:slot * 1024 + (i + 1) * P],
                            comb_rows[:, 8 * c + i, :].bitcast(F32), ident[:]))
                        if i == 7:
                            turned = pe(tr)
                        else:
                            pe.quiet(tr, r, slot_free)
                    o = act(lambda e, c=c, slot=slot: e.activation(
                        comb_t[:, c * 1024:(c + 1) * 1024], psum[:, slot * 1024:(slot + 1) * 1024], ACT.Copy), turned)
                    pairs.give(slot, o)
                    comb_done.append(o)
                units = F // E
                p = pool(lambda e: e.memset(pick_f[:].bitcast(F32), 0.0), start)
                for r0 in (0, E):
                    rows = pick_f[r0:r0 + E, :]
                    p = pool(lambda e, rows=rows: e.memset(rows.bitcast(F32), 1.0), p)
                    p = pool(lambda e, rows=rows: e.affine_select(
                        out=rows, in_=rows.bitcast(F32), compare_op=ALU.is_ge, fill=0.0, base=0,
                        pattern=[[1, F]], channel_multiplier=-units), p)
                    p = pool(lambda e, rows=rows: e.affine_select(
                        out=rows, in_=rows.bitcast(F32), compare_op=ALU.is_ge, fill=0.0, base=units - 1,
                        pattern=[[-1, F]], channel_multiplier=units), p)
                comb_done.append(p)

            banks = Ring(2)
            for slot in range(2):
                banks.give(slot, *pairs.readers)
            OUT = 6 * BANK
            out_free = [list(flat(o_banks.readers + pairs.readers))]
            bufs = Ring(2)
            pending = []
            work = []

            def down(item):
                n, c, j, slot, hi_ready, lo_ready = item
                f0, width, tiles, kind = groups[n]
                w_slot, _ = w_state[n]
                w_hi, w_lo = (p[0:width, w_slot, j * CH:(j + 1) * CH] for p in parts["down"])
                first, last = j == 0, j == tiles - 1
                for a, w, ready in ((hid_hi, w_hi, hi_ready), (hid_hi, w_lo, hi_ready), (hid_lo, w_hi, lo_ready)):
                    for i in range(4):
                        opens = first and w is w_hi and a is hid_hi and i % 2 == 0
                        closes = last and a is hid_lo
                        mm = (lambda e, a=a, w=w, i=i, opens=opens, closes=closes: e.matmul(
                            psum[:, OUT + i * CH:OUT + (i + 1) * CH], a[0:width, slot, i * P:(i + 1) * P], w,
                            start=opens, stop=closes, skip_group_check=True))
                        if a is hid_lo and i == 3:
                            done = pe(mm)
                        else:
                            pe.quiet(mm, ready, out_free[0] if first else None)
                bufs.give(slot, done)
                if last:
                    if n == len(groups) - 1 or c == 3:
                        pass
                    if c == 3:
                        w_free.give(w_slot, done)
                    xs = x[:, 4 * c:4 * c + 4, :]
                    if kind[0] == "scaled":
                        for i in range(4):
                            t = 4 * c + i
                            added = dve(lambda e, i=i, t=t: e.scalar_tensor_tensor(
                                x[:, t, :], psum[:, OUT + i * CH:OUT + (i + 1) * CH], coef[:, t, kind[1]:kind[1] + 1],
                                x[:, t, :], ALU.mult, ALU.add), done, coef_ready, x_ready[c])
                    else:
                        added = dve(lambda e: e.tensor_tensor(
                            xs.rearrange("p t n -> p (t n)"), psum[:, OUT:OUT + 1024],
                            xs.rearrange("p t n -> p (t n)"), ALU.add), done, x_ready[c])
                    out_free[0] = added
                    x_ready[c] = added

            for n, (f0, width, tiles, kind) in enumerate(groups):
                work += weight_work(n + 1) if n + 1 < len(groups) else []
                for c in range(4):
                    cols = slice(c * 512, (c + 1) * 512)
                    for j in range(tiles):
                        if c == 0 and j == 0:
                            pass
                        slot, free = banks.take()
                        b_slot, b_free = bufs.take()
                        base = slot * 3 * BANK
                        w_slot, w_ready = w_state[n]

                        def weights(name, k):
                            at = k * width * tiles + j * width
                            return tuple(p[:, w_slot, at:at + width] for p in parts[name])

                        rhs = [(xt_hi[:, k, cols], xt_lo[:, k, cols]) for k in range(KB)]
                        done = []
                        for i, name in enumerate(("gate", "up")):
                            todo = products(psum[0:width, base + i * BANK:base + (i + 1) * BANK],
                                            [weights(name, k) for k in range(KB)], rhs)
                            for mm in todo[:-1]:
                                pe.quiet(mm, free, w_ready, xt_done[c])
                            done.append(pe(todo[-1]))
                        g_ps, u_ps, c_ps = (psum[0:width, base + i * BANK:base + (i + 1) * BANK] for i in range(3))
                        sg, hd = silu[0:width, b_slot, :], hid[0:width, b_slot, :]
                        hh, hl = hid_hi[0:width, b_slot, :], hid_lo[0:width, b_slot, :]
                        r = act(lambda e, sg=sg, g_ps=g_ps: e.activation(sg, g_ps, ACT.Silu), done[0], b_free, start)
                        if kind[0] == "routed":
                            fs = slice(f0 + j * width, f0 + (j + 1) * width)
                            mix = pe(lambda e, c_ps=c_ps, fs=fs, cols=cols: e.matmul(
                                c_ps, pick_f[:, fs], comb_t[:, cols], start=True, stop=True), comb_done)
                            r = dve(lambda e, sg=sg, c_ps=c_ps: e.tensor_tensor(sg, c_ps, sg, ALU.mult), r, mix)
                        r = dve(lambda e, hd=hd, sg=sg, u_ps=u_ps: e.tensor_tensor(hd, u_ps, sg, ALU.mult),
                                r, done[1], b_free)
                        banks.give(slot, r)
                        hi = act(lambda e, hh=hh, hd=hd: e.activation(hh, hd, ACT.Copy), r, b_free)
                        lo = pool(lambda e, hh=hh, hd=hd, hl=hl: e.tensor_tensor(hl, hd, hh.bitcast(F32),
                                                                                 ALU.subtract), hi)
                        while pending:
                            down(pending.pop())
                        if work:
                            work.pop(0)()
                        pending.append((n, c, j, b_slot, hi, lo))
                while work:
                    work.pop(0)()
            while pending:
                down(pending.pop())
            pairs.readers[:] = [[(pe.sem, pe.count), (dve.sem, dve.count)]] * 3
            o_banks.readers[:] = [[(pe.sem, pe.count), (dve.sem, dve.count)]] * 2
            for c in range(4):
                x_ready[c] = layernorm(c, x_ready[c])
            s.close()

        attention(0, AttentionShape(16, softmax=False), None)
        experts(0, fence(), [(512 * n, P, 4, ("scaled", n // 2)) for n in range(4)], 2)
        attention(1, AttentionShape(32, softmax=True), fence())
        experts(1, fence(), [(512 * n, P, 4, ("routed",)) for n in range(6)] + [(3072, 96, 2, ("plain",))], 32)

        stored = sem("stored")
        for c in range(ALL_TILES // 4):
            sync.quiet(lambda e, c=c: e.dma_start(out_dram[:, 4 * c:4 * c + 4, :],
                                                  x[:, 4 * c:4 * c + 4, :]).then_inc(stored, 16), x_ready[c])

        block = ctx.enter_context(nc.Block())

        @block.sync
        def _(eng):
            sync.play(eng)
            eng.wait_ge(stored, 16 * (ALL_TILES // 4))

        block.tensor(pe.play)
        block.scalar(act.play)
        block.vector(dve.play)
        block.gpsimd(pool.play)


def rope_tables(base_freqs, angles, scale):
    c = np.cos(angles.astype(np.float64))
    s = np.sin(angles.astype(np.float64))
    cos = np.concatenate([c, c], -1)
    sin = np.concatenate([-s, s], -1)
    both = [np.stack([t * scale, t], 1).astype(np.float32) for t in (cos, sin)]
    return [np.ascontiguousarray(t.reshape(TILES, P, 2, -1).transpose(1, 0, 2, 3)) for t in both]


def constants():
    f32 = np.float32
    d0, d1 = CH // 16, CH // 32
    t = np.arange(SEQ, dtype=f32)
    inv0 = (1.0 / f32(10000.0) ** (np.arange(0, d0, 2, dtype=f32) / f32(d0))).astype(f32)
    cos0, sin0 = rope_tables(inv0, t[:, None] * inv0[None, :], 1.0)
    theta = (f32(10000.0) ** (-np.arange(0, d1, 2, dtype=f32) / f32(d1))).astype(f32)
    temporal = np.floor((np.arange(SEQ) // 72).astype(f32) * 0.5).astype(f32)
    angles = (t[:, None] * theta).astype(np.float64) + (temporal[:, None] * theta).astype(np.float64)
    cos1, sin1 = rope_tables(theta, angles, 1.0 / np.sqrt(d1))
    i = np.arange(P)
    return {
        "ident": np.eye(P, dtype=f32),
        "later": np.stack([np.where(i[None, :] > i[:, None], f32(MASKED), f32(0)),
                           np.where(i[None, :] < i[:, None], f32(MASKED), f32(0))], 1),
        "pick": np.eye(2, dtype=f32),
        "cos0": cos0, "sin0": sin0, "cos1": cos1, "sin1": sin1,
    }


def kernel(**inputs):
    import concourse.bacc as bacc
    from concourse.bass_utils import run_bass_kernel_spmd

    a = {k: np.asarray(v) for k, v in inputs.items()}
    width = a["L1_ffn_wd"].shape[0] * a["L1_ffn_wd"].shape[1]

    def by_channel(w):
        return w.transpose(1, 0, 2).reshape(CH, -1)

    arrays = {
        "x": a["L0_attn_x"],
        "wqkv0": a["L0_attn_w_qkv"], "wo0": a["L0_attn_w_out"],
        "ln_scale": a["L0_attn_ln_scale"], "ln_bias": a["L0_attn_ln_bias"],
        "router0": a["L0_ffn_gate_w"].T,
        "gate0": by_channel(a["L0_ffn_w_gate"].transpose(0, 2, 1)),
        "up0": by_channel(a["L0_ffn_w_up"].transpose(0, 2, 1)),
        "down0": a["L0_ffn_w_down"].transpose(0, 2, 1).reshape(-1, CH),
        "wqkv1": np.concatenate([a["L1_attn_Wq"].T, a["L1_attn_Wk"].T, a["L1_attn_Wv"].T], 1),
        "wo1": a["L1_attn_Wo"].T,
        "bias": np.concatenate([a["L1_attn_bq"], a["L1_attn_bk"], a["L1_attn_bv"], a["L1_attn_bo"]]),
        "router1": a["L1_ffn_gate_w"],
        "gate1": np.concatenate([by_channel(a["L1_ffn_wg"]), a["L1_ffn_sg"]], 1),
        "up1": np.concatenate([by_channel(a["L1_ffn_wu"]), a["L1_ffn_su"]], 1),
        "down1": np.concatenate([a["L1_ffn_wd"].reshape(width, CH), a["L1_ffn_sd"]], 0),
        **constants(),
    }
    nc = bacc.Bacc("TRN2", target_bir_lowering=False, num_devices=1)
    feeds, ins = {}, {}
    for name, value in arrays.items():
        value = np.ascontiguousarray(value)
        feeds[f"in_{name}"] = value
        ins[name] = nc.dram_tensor(f"in_{name}", value.shape, mybir.dt.from_np(value.dtype),
                                   kind="ExternalInput").ap()
    out = nc.dram_tensor("out", (BATCH, SEQ, CH), F32, kind="ExternalOutput").ap()
    build_program(nc, ins, out)
    result = run_bass_kernel_spmd(nc, [feeds], core_ids=[0])
    return result.results[0]["out"]
```

```python
from contextlib import ExitStack

import numpy as np
import concourse.bass as bass
from concourse import mybir

F32 = mybir.dt.float32
F32R = mybir.dt.float32r
BF16 = mybir.dt.bfloat16
ALU = mybir.AluOpType
ACT = mybir.ActivationFunctionType
X_AXIS = mybir.AxisListType.X
XY_AXES = mybir.AxisListType.XY

P = 128
BATCH, SEQ, CH = 2, 1024, 256
TILES = SEQ // P
ALL_TILES = BATCH * TILES
KB = CH // P
BANK = 512
QCH = 512
EPS = 1e-5
WEIGHTS_AHEAD = 2
MASKED = -1e30


class Engine:

    def __init__(self, sem, one_by_one=False):
        self.sem, self.count, self.queue = sem, 0, []
        self.one_by_one = one_by_one

    def __call__(self, issue, *waits):
        if self.one_by_one and self.count:
            waits += ((self.sem, self.count),)
        self.count += 1
        self.queue.append((issue, tuple(flat(waits)), True))
        return (self.sem, self.count)

    def quiet(self, issue, *waits):
        self.queue.append((issue, tuple(flat(waits)), False))

    def play(self, eng):
        reached = {}
        for issue, waits, signals in self.queue:
            for sem, value in waits:
                if reached.get(sem, 0) < value:
                    eng.wait_ge(sem, value)
                    reached[sem] = value
            inst = issue(eng)
            if signals:
                inst.then_inc(self.sem, 1)


def flat(waits):
    for w in waits:
        if w is None:
            continue
        if isinstance(w, list):
            yield from flat(w)
        else:
            yield w


class Ring:

    def __init__(self, n):
        self.readers, self.at = [None] * n, 0

    def take(self):
        slot = self.at
        self.at = (self.at + 1) % len(self.readers)
        return slot, self.readers[slot]

    def give(self, slot, *tokens):
        self.readers[slot] = list(tokens)


def copy_on_pool(eng, out, in_):
    return eng.tensor_scalar(out, in_, 1.0, 0.0, ALU.mult, ALU.add)


class AttentionShape:

    def __init__(self, heads, softmax):
        self.heads, self.softmax = heads, softmax
        self.d = CH // heads
        self.rows = 32 if softmax else 64
        self.heads_per_group = P // self.rows
        self.groups = heads // self.heads_per_group
        self.quads = heads // 4
        self.groups_per_quad = 4 // self.heads_per_group
        self.v_row = heads * (self.d + 1) + 32


def build_program(nc, ins, out):
    ctx = ExitStack()
    with ctx:
        def sb(name, shape, dt=F32, stack=ctx):
            return stack.enter_context(nc.sbuf_tensor(name, shape, dt))

        def sem(name):
            return ctx.enter_context(nc.semaphore(name))

        pe, act, dve = (Engine(sem(f"{n}_done")) for n in ("pe", "act", "dve"))
        pool = Engine(sem("pool_done"), one_by_one=True)
        sync = Engine(None)

        def load(name, dst, src, *waits):
            s = sem(f"loaded_{name}")
            sync.quiet(lambda e: e.dma_start(dst, src).then_inc(s, 16), *waits)
            return (s, 16)

        def fence():
            return [(e.sem, e.count) for e in (pe, act, dve, pool)]

        psum = ctx.enter_context(nc.psum_tensor("psum", [P, 8 * BANK], F32))
        pairs = Ring(3)
        o_read = [None, None]

        x = sb("x", [P, ALL_TILES, CH])
        stage = sb("stage", [P, 3072])
        ident = sb("ident", [P, P])
        ident_bf = sb("ident_bf", [P, P], BF16)
        later = sb("later", [P, 2, P])
        later_bf = sb("later_bf", [P, 2, P], BF16)
        ln_stats = sb("ln_stats", [P, ALL_TILES, 6])
        ln_mean_var = sb("ln_mean_var", [P, ALL_TILES, 2])
        ln_sd = sb("ln_sd", [P, ALL_TILES])
        ln_rstd = sb("ln_rstd", [P, ALL_TILES])

        x_dram = ins["x"].rearrange("b (t p) c -> p (b t) c", p=P)
        out_dram = out.rearrange("b (t p) c -> p (b t) c", p=P)
        ident_in = load("ident", ident[:], ins["ident"])
        x_ready = [None] * (ALL_TILES // 4)
        for c in range(ALL_TILES // 4):
            x_ready[c] = load(f"x{c}", x[:, 4 * c:4 * c + 4, :], x_dram[:, 4 * c:4 * c + 4, :])
        later_in = load("later", later[:], ins["later"])
        mask_ready = [dve(lambda e: e.tensor_copy(ident_bf[:], ident[:]), ident_in),
                      dve(lambda e: e.tensor_copy(later_bf[:], later[:]), later_in)]

        def split(src, hi, lo, src_ready, free=None):
            t = pool(lambda e: copy_on_pool(e, hi, src), src_ready, free)
            return pool(lambda e: e.tensor_tensor(lo, src, hi.bitcast(F32), ALU.subtract), t)

        def products(dst, lhs, rhs, last=True, first=True):
            terms = []
            for (lh, ll), (rh, rl) in zip(lhs, rhs):
                terms += [(lh, rh), (lh, rl), (ll, rh)]
            return [(lambda e, a=a, b=b, s=first and i == 0, z=last and i == len(terms) - 1:
                     e.matmul(dst, a, b, start=s, stop=z)) for i, (a, b) in enumerate(terms)]

        def to_channels(src, hi, lo, src_ready, free):
            slot, slot_free = pairs.take()
            bank = psum[:, slot * 1024:(slot + 1) * 1024].rearrange("p (k n) -> p k n", k=KB)
            for k in range(KB):
                for i in range(4):
                    t = (lambda e, k=k, i=i, tile=src(i): e.transpose(
                        bank[:, k, i * P:(i + 1) * P], tile[:, k * P:(k + 1) * P], ident[:]))
                    if (k, i) == (KB - 1, 3):
                        turned = pe(t)
                    else:
                        pe.quiet(t, src_ready, slot_free, ident_in)
            hi_done = act(lambda e: e.activation(hi, bank, ACT.Copy), turned, free)
            lo_done = dve(lambda e: e.tensor_tensor(lo, bank, hi.bitcast(F32), ALU.subtract),
                          hi_done, free)
            pairs.give(slot, lo_done)
            return [hi_done, lo_done]

        def layernorm(c, ready):
            t0, t1 = 4 * c, 4 * c + 4
            stats = [dve(lambda e, t=t: e.bn_stats(ln_stats[:, t, :], x[:, t, :]), ready)
                     for t in range(t0, t1)]
            for t in range(t0, t1):
                moments = dve(lambda e, t=t: e.bn_aggr(ln_mean_var[:, t, :], ln_stats[:, t, :]), stats[-1])
            sd = dve(lambda e: e.tensor_scalar(ln_sd[:, t0:t1], ln_mean_var[:, t0:t1, 1], EPS, None,
                                               ALU.add), moments)
            sd = act(lambda e: e.activation(ln_sd[:, t0:t1], ln_sd[:, t0:t1], ACT.Sqrt), sd)
            rstd = dve(lambda e: e.reciprocal(ln_rstd[:, t0:t1], ln_sd[:, t0:t1]), sd)
            done = [dve(lambda e, t=t: e.tensor_scalar(x[:, t, :], x[:, t, :], ln_mean_var[:, t, 0:1],
                                                       ln_rstd[:, t:t + 1], ALU.subtract, ALU.mult), rstd)
                    for t in range(t0, t1)]
            return done[-1]

        def zero(dst, *waits):
            rows, n = dst.shape
            return act(lambda e: e.activation(dst, ident[0:rows, 0:1].to_broadcast([rows, n]), ACT.Copy, scale=0.0),
                       ident_in, *waits)

        stage_free = [None]

        def attention(layer, shape, start):
            s = ExitStack()
            H, d, R = shape.heads, shape.d, shape.rows
            HG = shape.heads_per_group

            def buf(name, sh, dt=F32):
                return sb(f"{name}{layer}", sh, dt, s)

            w_hi = buf("wqkv_hi", [P, KB, 3 * CH], F32R)
            w_lo = buf("wqkv_lo", [P, KB, 3 * CH], F32R)
            wo_hi = buf("wo_hi", [P, KB, CH], F32R)
            wo_lo = buf("wo_lo", [P, KB, CH], F32R)
            cos = buf("cos", [P, TILES, 2, d])
            sin = buf("sin", [P, TILES, 2, d])
            qk = buf("qk", [P, TILES, 2, CH])
            v = buf("v", [P, TILES, shape.v_row])
            xt = buf("xt", [P, 2 * KB * SEQ], F32R)
            xt_hi = xt[:, 0:KB * SEQ].rearrange("p (k n) -> p k n", k=KB)
            xt_lo = xt[:, KB * SEQ:].rearrange("p (k n) -> p k n", k=KB)
            q_rows = buf("q_rows", [P, 2, TILES * P], F32R)
            k_rows = buf("k_rows", [P, 1, TILES * P], F32R)
            qt = buf("qt", [P, 4, SEQ], F32R)
            kt = buf("kt", [P, SEQ])
            km = buf("km", [P, 2, 4, SEQ], F32R)
            probs = buf("probs", [P, WEIGHTS_AHEAD + 2, 4, QCH])
            o_cols = buf("o_cols", [P, 2, SEQ])
            ao = buf("ao", [P, TILES, CH])
            o_rcp = buf("o_rcp", [P, 2, TILES, 4])

            ROTATING = 6

            def rotated(u, which):
                return probs[:, u // 2, 2 * (u % 2) + which, :]

            def masked_k(slot):
                return km[:, slot] if slot < 2 else xt[:, :].rearrange("p (h n) -> p h n", h=4)

            def pieces(rows, slot):
                return rows[:, slot, :].rearrange("p (t h f) -> p t h f", t=TILES, h=HG)

            w_in = load(f"wqkv{layer}", stage[:, 0:KB * 3 * CH].rearrange("p (k n) -> p k n", k=KB),
                        ins[f"wqkv{layer}"].rearrange("(k p) n -> p k n", p=P), stage_free[0])
            wo_in = load(f"wo{layer}", stage[:, KB * 3 * CH:KB * 4 * CH].rearrange("p (k n) -> p k n", k=KB),
                         ins[f"wo{layer}"].rearrange("(k p) n -> p k n", p=P), stage_free[0])
            cos_in = load(f"cos{layer}", cos[:], ins[f"cos{layer}"], start)
            sin_in = load(f"sin{layer}", sin[:], ins[f"sin{layer}"], start)
            w_ready = split(stage[:, 0:KB * 3 * CH], w_hi[:, :, :].rearrange("p k n -> p (k n)"),
                            w_lo[:, :, :].rearrange("p k n -> p (k n)"), w_in, start)
            wo_ready = split(stage[:, KB * 3 * CH:KB * 4 * CH], wo_hi[:, :, :].rearrange("p k n -> p (k n)"),
                             wo_lo[:, :, :].rearrange("p k n -> p (k n)"), wo_in, start)
            stage_free[0] = wo_ready
            v_ones = pool(lambda e: e.memset(v[:], 1.0), start)
            rows_clear = [dve(lambda e: e.memset(q_rows[:].bitcast(F32), 0.0), start),
                          dve(lambda e: e.memset(k_rows[:].bitcast(F32), 0.0), start),
                          [zero(km[:, i, h, :], start) for i in range(2) for h in range(4)]]
            if shape.softmax:
                rows_clear.append(dve(lambda e: e.memset(
                    pieces(k_rows, 0)[:, :, :, 3 * d:3 * d + 2].bitcast(F32), 1.0), rows_clear[1]))
                neg_max = buf("neg_max", [P, 2, TILES, 4])
                flat_ao = ao[0:2].rearrange("p t n -> p (t n)")
                bias, bias_low = flat_ao[:, 0:4 * CH], flat_ao[:, 4 * CH:8 * CH]
                bias_rows = buf("bias_rows", [2, 4 * CH], F32R)
                pick = buf("pick", [2, 2])
                ones_f = buf("ones_f", [2, P])
                ones = buf("ones", [2, P], F32R)
                b_in = [load(f"bias{r}", bias[r:r + 1, :], ins["bias"].rearrange("(a n) -> a n", a=1), start)
                        for r in range(2)]
                b_in.append(load("pick", pick[:], ins["pick"], start))
                b = dve(lambda e: e.tensor_copy(bias_rows[:], bias), b_in)
                b = dve(lambda e: e.tensor_tensor(bias_low, bias, bias_rows[:].bitcast(F32), ALU.subtract), b)
                b = dve(lambda e: e.tensor_scalar(bias_low, bias_low, pick[:, 1:2], None, ALU.mult), b)
                b = dve(lambda e: e.scalar_tensor_tensor(bias_rows[:], bias_rows[:].bitcast(F32), pick[:, 0:1],
                                                         bias_low, ALU.mult, ALU.add), b)
                o = dve(lambda e: e.memset(ones_f[:], 1.0), start)
                bias_ready = [b, dve(lambda e: e.tensor_copy(ones[:], ones_f[:]), o)]
            else:
                qk_scale = buf("qk_scale", [P, d])
                qk_bias = buf("qk_bias", [P, d])
                scale_in = load("qk_scale", qk_scale[:], ins["ln_scale"].partition_broadcast(P), start)
                shift_in = load("qk_bias", qk_bias[:], ins["ln_bias"].partition_broadcast(P), start)
                mom = buf("mom", [P, ROTATING, 4, 2 * H])
                bias_ready = None

            q_taken = Ring(2)
            k_read, kt_read = [None, None], [None, None]
            qt_taken = Ring(4) if not shape.softmax else (Ring(2), Ring(2))
            km_taken = Ring(3 if shape.softmax else 2)
            p_taken = Ring(WEIGHTS_AHEAD + 2)
            oc_taken = Ring(2)

            def x_to_channels(b, c, free):
                cols = slice(c * 512, (c + 1) * 512)
                return to_channels(lambda i: x[:, b * TILES + 4 * c + i, :], xt_hi[:, :, cols], xt_lo[:, :, cols],
                                   x_ready[2 * b + c], free)

            norms_due = []
            for b in range(BATCH):
                before = before_next if b else start
                km_taken.at = 0

                xt_done = [x_to_channels(b, 0, before) if b == 0 else first_chunk, x_to_channels(b, 1, before)]
                v_done, qk_done = [], [None] * TILES
                chain = {}

                def project(t):
                    slot, slot_free = pairs.take()
                    base = slot * 1024
                    cols = slice(t * P, (t + 1) * P)
                    first = True
                    for k in range(KB):
                        for a, w in ((xt_hi, w_hi), (xt_hi, w_lo), (xt_lo, w_hi)):
                            end = k == KB - 1 and a is xt_lo and not shape.softmax
                            pe.quiet(lambda e, a=a, w=w, k=k, f=first, z=end: e.matmul(
                                psum[:, base:base + 512], a[:, k, cols], w[:, k, 0:512], start=f, stop=z),
                                xt_done[t // 4], slot_free, w_ready)
                            mm = (lambda e, a=a, w=w, k=k, f=first, z=end: e.matmul(
                                psum[:, base + 512:base + 768], a[:, k, cols], w[:, k, 512:768], start=f, stop=z))
                            first = False
                            if end:
                                projected = pe(mm)
                            else:
                                pe.quiet(mm)
                    if shape.softmax:
                        pe.quiet(lambda e: e.matmul(psum[:, base:base + 512], ones[:], bias_rows[:, 0:512],
                                                    start=False, stop=True), bias_ready)
                        projected = pe(lambda e: e.matmul(psum[:, base + 512:base + 768], ones[:],
                                                          bias_rows[:, 512:768], start=False, stop=True))
                    vv = v[:, t, 0:H * (d + 1)].rearrange("p (h e) -> p h e", h=H)[:, :, 0:d]
                    v_out = act(lambda e: e.activation(
                        vv, psum[:, base + 512:base + 768].rearrange("p (h e) -> p h e", h=H), ACT.Copy),
                        projected, v_ones, before)
                    v_done.append(v_out)

                    u = t % ROTATING
                    pq = psum[:, base:base + 512].rearrange("p (s h e) -> p s h e", s=2, h=H)
                    ra = rotated(u, 0).rearrange("p (s h e) -> p s h e", s=2, h=H)
                    rb = rotated(u, 1).rearrange("p (s h e) -> p s h e", s=2, h=H)
                    h2 = d // 2

                    def table(tb, lo, hi):
                        return tb[:, t, :, lo:hi].unsqueeze(2).to_broadcast([P, 2, H, hi - lo])

                    free = [before, chain.get(("free", u))]
                    a1 = dve(lambda e: e.tensor_tensor(ra, pq, table(cos, 0, d), ALU.mult),
                             projected, cos_in, free)
                    dve(lambda e: e.tensor_tensor(rb[:, :, :, 0:h2], pq[:, :, :, h2:d], table(sin, 0, h2),
                                                  ALU.mult), sin_in)
                    b2 = dve(lambda e: e.tensor_tensor(rb[:, :, :, h2:d], pq[:, :, :, 0:h2],
                                                       table(sin, h2, d), ALU.mult))
                    pairs.give(slot, v_out, b2)
                    if shape.softmax:
                        done = dve(lambda e: e.tensor_tensor(qk[:, t].rearrange("p s (h e) -> p s h e", h=H),
                                                             ra, rb, ALU.add), b2)
                        qk_done[t] = done
                        chain["free", u] = done
                        return
                    ra2 = rotated(u, 0).rearrange("p (g e) -> p g e", e=d)
                    rb2 = rotated(u, 1).rearrange("p (g e) -> p g e", e=d)
                    m = mom[:, u]
                    r = dve(lambda e: e.tensor_tensor(rotated(u, 0), rotated(u, 0), rotated(u, 1), ALU.add), b2)
                    r = dve(lambda e: e.tensor_reduce(m[:, 0], ra2, X_AXIS, ALU.add), r)
                    r = dve(lambda e: e.tensor_scalar(m[:, 0], m[:, 0], 1.0 / d, None, ALU.mult), r)
                    r = dve(lambda e: e.tensor_tensor(ra2, ra2, m[:, 0].unsqueeze(2).to_broadcast([P, 2 * H, d]),
                                                      ALU.subtract), r)
                    chain["sq", t] = act(lambda e: e.activation(rb2, ra2, ACT.Square), r)

                def spread(t):
                    u = t % ROTATING
                    m = mom[:, u]
                    rb2 = rotated(u, 1).rearrange("p (g e) -> p g e", e=d)
                    r = dve(lambda e: e.tensor_reduce(m[:, 1], rb2, X_AXIS, ALU.add), chain["sq", t])
                    r = dve(lambda e: e.tensor_scalar(m[:, 1], m[:, 1], 1.0 / d, EPS, ALU.mult, ALU.add), r)
                    chain["sd", t] = act(lambda e: e.activation(m[:, 2], m[:, 1], ACT.Sqrt), r)

                def scale(t):
                    u = t % ROTATING
                    m = mom[:, u]
                    ra2 = rotated(u, 0).rearrange("p (g e) -> p g e", e=d)
                    r = dve(lambda e: e.reciprocal(m[:, 3], m[:, 2]), chain["sd", t])
                    r = pool(lambda e: e.tensor_tensor(ra2, ra2, m[:, 3].unsqueeze(2).to_broadcast([P, 2 * H, d]),
                                                       ALU.mult), r)
                    r = pool(lambda e: e.tensor_tensor(ra2, ra2, qk_scale[:].unsqueeze(1).to_broadcast([P, 2 * H, d]),
                                                       ALU.mult), r, scale_in)
                    done = pool(lambda e: e.tensor_tensor(
                        qk[:, t].rearrange("p s (h e) -> p (s h) e", h=H), ra2,
                        qk_bias[:].unsqueeze(1).to_broadcast([P, 2 * H, d]), ALU.add), r, shift_in, before)
                    qk_done[t] = done
                    chain["free", u] = done

                group_ready, qt_ready, km_ready = {}, {}, {}

                def cut_pieces(g, t0=0, t1=TILES, hurry=False):
                    if t0 == 0:
                        group_ready[g] = [*q_taken.take(), None]
                    slot, free = group_ready[g][0:2]
                    hd = slice(g * HG * d, (g + 1) * HG * d)

                    def src(which):
                        return qk[:, t0:t1, which, hd].rearrange("p t (h e) -> p t h e", h=HG)

                    def put(rows, at):
                        return pieces(rows, slot if rows is q_rows else 0)[:, t0:t1, :, at * d:(at + 1) * d]

                    def copy(dst, src, *waits):
                        if hurry:
                            return act(lambda e: e.activation(dst, src, ACT.Copy), *waits)
                        return pool(lambda e: copy_on_pool(e, dst, src), *waits)

                    hi_at = ((0, 1), (0, 2))
                    lo_at = ((2,), (1,)) if shape.softmax else ((2, 3), (1, 3))
                    waits = [qk_done[t0:t1], rows_clear, free, k_read[t0 // 4:t1 // 4]]
                    done = []
                    for which, rows in ((0, q_rows), (1, k_rows)):
                        hi = copy(put(rows, hi_at[which][0]), src(which), waits)
                        low = (dve if hurry else pool)(lambda e, w=which, r=rows: e.tensor_tensor(
                            put(r, lo_at[w][0]), src(w), put(r, hi_at[w][0]).bitcast(F32), ALU.subtract),
                            hi, waits)
                        hi = copy(put(rows, hi_at[which][1]), src(which), waits)
                        last = [hi, low]
                        if not shape.softmax:
                            last.append(copy(put(rows, 3), put(rows, lo_at[which][0]).bitcast(F32), low))
                        elif which == 0:
                            last.append((dve if hurry else pool)(lambda e: e.memset(
                                pieces(q_rows, slot)[:, t0:t1, :, 3 * d:3 * d + 2].bitcast(F32), 0.0), waits))
                        done.append(last)
                    group_ready[g][2] = done

                def turn_pieces(g, t0=0, t1=TILES):
                    slot, _, done = group_ready[g]
                    cols = slice(t0 * P, t1 * P)

                    def turn(rows, at, ready):
                        pair, pair_free = pairs.take()
                        for t in range(t0, t1):
                            tr = (lambda e, t=t: e.transpose(
                                psum[:, pair * 1024 + (t - t0) * P:pair * 1024 + (t - t0 + 1) * P],
                                rows[:, at, t * P:(t + 1) * P].bitcast(F32), ident[:]))
                            if t == t1 - 1:
                                turned = pe(tr)
                            else:
                                pe.quiet(tr, ready, pair_free)
                        return pair, psum[:, pair * 1024:pair * 1024 + (t1 - t0) * P], turned

                    if t0 == 0:
                        q_slot, q_free = (qt_taken[0] if shape.softmax else qt_taken).take()
                        qt_ready[g] = (q_slot, [q_free])
                    q_slot, q_ready = qt_ready[g]
                    pair, at, turned = turn(q_rows, slot, done[0])
                    q_out = act(lambda e, at=at: e.activation(qt[:, q_slot, cols], at, ACT.Copy),
                                turned, q_ready[0], before)
                    pairs.give(pair, q_out)
                    q_ready.append(q_out)
                    pair, at, turned = turn(k_rows, 0, done[1])
                    for half in range(t0 // 4, t1 // 4):
                        k_read[half] = turned
                    if not shape.softmax and t1 == TILES:
                        q_taken.give(slot, turned)
                    k_out = act(lambda e, at=at: e.activation(kt[:, cols], at, ACT.Copy),
                                turned, kt_read[t0 // 4:t1 // 4], before)
                    pairs.give(pair, k_out)
                    quad, part = divmod(g, shape.groups_per_quad)
                    if part == 0 and t0 == 0:
                        m_slot, m_free = km_taken.take()
                        km_ready[quad] = [m_slot, m_free]
                    m_slot, m_free = km_ready[quad][0:2]
                    for h in range(HG):
                        r = slice(h * R, (h + 1) * R)
                        m_out = pool(lambda e, h=h, r=r: copy_on_pool(
                            e, masked_k(m_slot)[r, part * HG + h, cols], kt[r, cols]), k_out, m_free, rows_clear)
                    km_ready[quad].append(m_out)
                    for half in range(t0 // 4, t1 // 4):
                        kt_read[half] = m_out

                max_done = {}

                def max_units(g):
                    units = []
                    for i in range(TILES):
                        w = (i + 1) * P
                        per = 4 if w <= 256 else 2 if w <= 512 else 1
                        for h0 in range(0, 4, per):
                            units.append((i, w, h0, per))
                    return units

                def max_unit(g, unit):
                    i, w, h0, n = unit
                    slot, slot_free = pairs.take()
                    base = slot * 1024
                    q_slot, q_ready = qt_ready[g]
                    keys = masked_k(km_ready[g][0])
                    waits = [slot_free, q_ready, km_ready[g][2:], mask_ready]
                    q_cols = qt[:, q_slot, i * P:(i + 1) * P]
                    if w <= 256:
                        per, part, stride = 512 // w, w, w
                    elif w <= 512:
                        per, part, stride = 1, w, 512
                    else:
                        per, part, stride = 1, w // 2, 512
                    halves = w // part
                    for h in range(h0, h0 + n, per):
                        for c0 in range(0, w, part):
                            at = base + ((h - h0) * halves + c0 // part) * stride
                            last = c0 + part == w
                            pe.quiet(lambda e, h=h, at=at, c0=c0, z=not last: e.matmul(
                                psum[:, at:at + per * part].rearrange("p (h n) -> p h n", h=per), q_cols,
                                keys[:, h:h + per, c0:c0 + part], start=True, stop=z), waits)
                            if last:
                                dst = psum[:, at:at + per * part].rearrange(
                                    "p (h n) -> p h n", h=per)[:, :, part - P:part]
                                mm = (lambda e, dst=dst: e.matmul(
                                    dst, ident_bf[:], later_bf[:, 0, :].unsqueeze(1).to_broadcast([P, per, P]),
                                    start=False, stop=True))
                                if h == h0 + n - per:
                                    scored = pe(mm)
                                else:
                                    pe.quiet(mm)
                    view = psum[:, base:base + n * halves * stride].rearrange(
                        "p (h s n) -> p h s n", h=n, s=halves)[:, :, :, 0:part]
                    m = dve(lambda e: e.tensor_reduce(neg_max[:, g % 2, i, h0:h0 + n], view, XY_AXES, ALU.max,
                                                      negate=True), scored, max_done.get(("read", g - 2)), before)
                    pairs.give(slot, m)
                    max_done[g, i] = m
                    if i == TILES - 1 and h0 == 3:
                        qt_taken[0].give(q_slot, scored)

                def cut_max(g, half):
                    slot = group_ready[g][0]
                    t0, t1 = half * 4, half * 4 + 4
                    nm = neg_max[:, g % 2, t0:t1, :].unsqueeze(3)
                    at = pieces(q_rows, slot)[:, t0:t1, :, 3 * d:3 * d + 1]
                    at_lo = pieces(q_rows, slot)[:, t0:t1, :, 3 * d + 1:3 * d + 2]
                    m = pool(lambda e: copy_on_pool(e, at, nm), max_done[g, t1 - 1])
                    m = pool(lambda e: e.tensor_tensor(at_lo, nm, at.bitcast(F32), ALU.subtract), m)
                    if half:
                        max_done["read", g] = m
                    max_done["cut", g, half] = m

                def turn_max(g, half):
                    slot, m = group_ready[g][0], max_done["cut", g, half]
                    t0, t1 = half * 4, half * 4 + 4
                    pair, pair_free = pairs.take()
                    for t in range(t0, t1):
                        tr = (lambda e, t=t: e.transpose(
                            psum[:, pair * 1024 + (t - t0) * P:pair * 1024 + (t - t0 + 1) * P],
                            q_rows[:, slot, t * P:(t + 1) * P].bitcast(F32), ident[:]))
                        if t == t1 - 1:
                            turned = pe(tr)
                        else:
                            pe.quiet(tr, m, pair_free)
                    if half:
                        q_taken.give(slot, turned)
                    if half == 0:
                        q_slot, q_free = qt_taken[1].take()
                        qt_ready["max", g] = [q_slot, q_free]
                    q_slot, q_free = qt_ready["max", g][0:2]
                    q_out = act(lambda e: e.activation(qt[:, 2 + q_slot, half * 512:(half + 1) * 512],
                                                       psum[:, pair * 1024:pair * 1024 + 512], ACT.Copy),
                                turned, q_free, before)
                    pairs.give(pair, q_out)
                    qt_ready["max", g].append(q_out)

                weighed = []
                o_turn = {}

                def weigh(step):
                    quad, c, key, q0, w, slot, ready = step
                    bank = (6 + c) * BANK
                    bank_free = o_read[c] if key == 0 else None
                    for h in range(4):
                        at = (4 * quad + h) * (d + 1)
                        mm = (lambda e, h=h, at=at: e.matmul(
                            psum[32 * h:32 * h + 32, bank + q0:bank + QCH], v[:, key, at:at + 32],
                            probs[:, slot, h, 0:w], start=(key == 0), stop=(key == 4 * c + 3)))
                        if h == 3:
                            done = pe(mm)
                        else:
                            pe.quiet(mm, ready, bank_free, v_done)
                    p_taken.give(slot, done)
                    if key == 4 * c + 3:
                        if c == 0:
                            o_turn[quad] = list(oc_taken.take())
                        oc, oc_free = o_turn[quad][0:2]
                        o_out = act(lambda e: e.activation(o_cols[:, oc, c * QCH:(c + 1) * QCH],
                                                           psum[:, bank:bank + QCH], ACT.Copy), done, oc_free)
                        o_turn[quad].append(o_out)
                        o_read[c] = o_out

                def weights_step(quad, c, key):
                    j = key - 4 * c
                    q0 = max(j, 0) * P
                    w = QCH - q0
                    per = 2 if w > 256 else 4
                    keys = masked_k(km_ready[quad][0])
                    masks = j >= 0 and shape.softmax
                    p_slot, p_free = p_taken.take()
                    ready = []
                    for h0 in range(0, 4, per):
                        slot, slot_free = pairs.take()
                        base = slot * 1024
                        early = max(0, 256 - w)
                        stride = 512 if per == 2 else w + early
                        for h in range(h0, h0 + per):
                            if shape.softmax:
                                q_slot, q_ready = 2 + qt_ready["max", quad][0], qt_ready["max", quad][2 + c]
                            else:
                                q_slot, q_ready = qt_ready[2 * quad + h // 2]
                            at = base + (h - h0) * stride
                            mm = (lambda e, h=h, at=at, q_slot=q_slot: e.matmul(
                                psum[:, at:at + early + w], keys[:, h, key * P:(key + 1) * P],
                                qt[:, q_slot, c * QCH + q0 - early:(c + 1) * QCH], start=True, stop=not masks))
                            if masks:
                                pe.quiet(mm, slot_free, q_ready, km_ready[quad][2:])
                                mm = (lambda e, at=at: e.matmul(psum[:, at + early:at + early + P], ident_bf[:], later_bf[:, 1, :],
                                                                start=False, stop=True))
                            if h == h0 + per - 1:
                                scored = pe(mm, q_ready)
                            else:
                                pe.quiet(mm, slot_free, q_ready, km_ready[quad][2:])
                        view = psum[:, base:base + per * stride].rearrange("p (h n) -> p h n", h=per)[
                            :, :, early:early + w]
                        dst = probs[:, p_slot, h0:h0 + per, 0:w]
                        t = act(lambda e, view=view, dst=dst: e.activation(
                            dst, view, ACT.Exp if shape.softmax else ACT.Square), scored, p_free, qk_done)
                        pairs.give(slot, t)
                        if not shape.softmax:
                            where = pool if (key + h0 // 2) % 4 == 3 and j < 0 else dve
                            t = where(lambda e, dst=dst: e.tensor_tensor(dst, dst, dst, ALU.mult), t)
                        ready.append(t)
                    if j >= 0 and not shape.softmax:
                        dst = probs[:, p_slot, :, 0:P]
                        ready.append(pool(lambda e: e.affine_select(
                            out=dst, in_=dst, compare_op=ALU.is_ge, fill=0.0, base=0,
                            pattern=[[0, 4], [1, P]], channel_multiplier=-1), ready[:]))
                    if key == 4 * c + 3 and c == 1:
                        km_taken.give(km_ready[quad][0], scored)
                        if shape.softmax:
                            qt_taken[1].give(qt_ready["max", quad][0], scored)
                        else:
                            for g in (2 * quad, 2 * quad + 1):
                                qt_taken.give(qt_ready[g][0], scored)
                    weighed.append((quad, c, key, q0, w, p_slot, ready))
                    if len(weighed) > WEIGHTS_AHEAD:
                        weigh(weighed.pop(0))

                def normalize(quad, t0=0, t1=TILES):
                    while weighed and weighed[0][0] == quad and weighed[0][1] * 4 < t1:
                        weigh(weighed.pop(0))
                    oc = o_turn[quad][0]
                    pair, pair_free = pairs.take()
                    for t in range(t0, t1):
                        tr = (lambda e, t=t: e.transpose(
                            psum[:, pair * 1024 + (t - t0) * P:pair * 1024 + (t - t0 + 1) * P],
                            o_cols[:, oc, t * P:(t + 1) * P], ident[:]))
                        if t == t1 - 1:
                            turned = pe(tr)
                        else:
                            pe.quiet(tr, o_turn[quad][2:], pair_free)
                    if t1 == TILES:
                        oc_taken.give(oc, turned)
                    o = psum[:, pair * 1024:pair * 1024 + (t1 - t0) * P].rearrange("p (t h e) -> p t h e", t=t1 - t0, h=4)
                    rcp = o_rcp[:, quad % 2, t0:t1].unsqueeze(3)
                    r = dve(lambda e: e.reciprocal(rcp, o[:, :, :, d:d + 1]), turned, before)
                    dst = ao[:, t0:t1, quad * 4 * d:(quad + 1) * 4 * d].rearrange("p t (h e) -> p t h e", h=4)
                    done = dve(lambda e: e.tensor_tensor(
                        dst, o[:, :, :, 0:d], rcp.to_broadcast([P, t1 - t0, 4, d]), ALU.mult), r)
                    pairs.give(pair, done)
                    return done

                turned_out = {}

                def turn_out(c, ready):
                    cols = slice(c * 512, (c + 1) * 512)
                    turned_out[c] = to_channels(lambda i: ao[:, 4 * c + i, :], xt_hi[:, :, cols], xt_lo[:, :, cols],
                                                ready, (pe.sem, pe.count))

                def project_out(c):
                    slot, slot_free = pairs.take()
                    base = slot * 1024
                    for i in range(4):
                        dst = psum[:, base + i * CH:base + (i + 1) * CH]
                        tk = slice((4 * c + i) * P, (4 * c + i + 1) * P)
                        todo = products(dst, [(xt_hi[:, k, tk], xt_lo[:, k, tk]) for k in range(KB)],
                                        [(wo_hi[:, k, :], wo_lo[:, k, :]) for k in range(KB)],
                                        last=not shape.softmax)
                        if shape.softmax:
                            todo.append(lambda e, dst=dst: e.matmul(dst, ones[:], bias_rows[:, 3 * CH:4 * CH],
                                                                    start=False, stop=True))
                        for mm in todo[:-1]:
                            pe.quiet(mm, turned_out[c], slot_free, wo_ready)
                        projected = pe(todo[-1])
                    g = 2 * b + c
                    xs = x[:, 4 * g:4 * g + 4, :].rearrange("p t n -> p (t n)")
                    added = dve(lambda e: e.tensor_tensor(xs, psum[:, base:base + 1024], xs, ALU.add),
                                projected, x_ready[g])
                    pairs.give(slot, added)
                    x_ready[g] = added
                    norms_due.append(g)

                HALF = TILES // 2

                def first_max(i0, i1):
                    for unit in max_units(0):
                        if i0 <= unit[0] < i1:
                            max_unit(0, unit)

                for t in range(TILES + 2):
                    if t < TILES:
                        project(t)
                    if not shape.softmax:
                        if 1 <= t <= TILES:
                            spread(t - 1)
                        if 2 <= t:
                            scale(t - 2)
                    if shape.softmax and t == HALF + 1:
                        cut_pieces(0, 0, HALF, hurry=True)
                        turn_pieces(0, 0, HALF)
                    if shape.softmax and HALF + 1 < t < TILES:
                        first_max(2 * (t - HALF - 2), 2 * (t - HALF - 1))
                projected_all = (pe.sem, pe.count)
                while norms_due:
                    g = norms_due.pop()
                    x_ready[g] = layernorm(g, x_ready[g])
                if shape.softmax:
                    cut_pieces(0, HALF, TILES, hurry=True)
                    turn_pieces(0, HALF, TILES)
                    km_taken.give(2, [zero(masked_k(2)[:, h, :], projected_all) for h in range(4)])
                    cut_pieces(1)
                    turn_pieces(1)
                    first_max(HALF, TILES)
                    cut_max(0, 0)
                    turn_max(0, 0)
                else:
                    for g in (0, 1):
                        cut_pieces(g, hurry=True)
                        turn_pieces(g)
                for quad in range(shape.quads):
                    steps = [(c, key) for c in range(SEQ // QCH) for key in range(4 * c + 4)]
                    between = []
                    if quad:
                        between.append((3, lambda q=quad - 1: normalize(q)))
                    if shape.softmax:
                        between.append((0, lambda q=quad: cut_max(q, 1)))
                        between.append((2, lambda q=quad: turn_max(q, 1)))
                        if quad + 2 < shape.quads:
                            between.append((4, lambda q=quad + 2: cut_pieces(q)))
                            between.append((9, lambda q=quad + 2: turn_pieces(q)))
                        if quad + 1 < shape.quads:
                            units = max_units(quad + 1)
                            for n, unit in enumerate(units):
                                between.append((0.5 + n * 11.5 / len(units),
                                                lambda q=quad + 1, unit=unit: max_unit(q, unit)))
                            between.append((7, lambda q=quad + 1: cut_max(q, 0)))
                            between.append((10, lambda q=quad + 1: turn_max(q, 0)))
                    elif quad + 1 < shape.quads:
                        between.append((0, lambda q=quad: cut_pieces(2 * q + 2)))
                        between.append((3, lambda q=quad: turn_pieces(2 * q + 2)))
                        between.append((3, lambda q=quad: cut_pieces(2 * q + 3)))
                        between.append((7, lambda q=quad: turn_pieces(2 * q + 3)))
                    if quad == shape.quads - 1:
                        between.append((7, lambda q=quad: turned_out.update(ready=normalize(q, 0, HALF))))
                        between.append((9, lambda: turn_out(0, turned_out["ready"])))
                        between.append((11, lambda: project_out(0)))
                    between.sort(key=lambda p: p[0])
                    for n, (c, key) in enumerate(steps):
                        while between and between[0][0] <= n:
                            between.pop(0)[1]()
                        weights_step(quad, c, key)
                    for _, what in between:
                        what()
                while weighed:
                    weigh(weighed.pop(0))
                before_next = fence()
                turn_out(1, normalize(shape.quads - 1, HALF, TILES))
                if b + 1 < BATCH:
                    first_chunk = x_to_channels(b + 1, 0, (pe.sem, pe.count))
                project_out(1)
                before_next += fence()
            laid_anew = fence()
            for g in norms_due:
                x_ready[g] = layernorm(g, x_ready[g])
            s.close()
            return laid_anew

        w_loads = [sem("loaded_weights"), 0]

        def experts(layer, start, groups, n_experts):
            s = ExitStack()

            def buf(name, sh, dt=F32):
                return sb(f"{name}{layer}", sh, dt, s)

            T = BATCH * SEQ
            xt_hi = buf("fxt_hi", [P, KB, T], F32R)
            xt_lo = buf("fxt_lo", [P, KB, T], F32R)
            parts = {n: (buf(f"{n}_hi", [P, 2, 1024], F32R), buf(f"{n}_lo", [P, 2, 1024], F32R))
                     for n in ("gate", "up", "down")}
            silu = buf("silu", [P, 2, 512])
            hid = buf("hid", [P, 2, 512])
            hid_hi = buf("hid_hi", [P, 2, 512], F32R)
            hid_lo = buf("hid_lo", [P, 2, 512], F32R)
            gw = buf("gw", [P, KB, n_experts])
            gw_hi = buf("gw_hi", [P, KB, n_experts], F32R)
            gw_lo = buf("gw_lo", [P, KB, n_experts], F32R)
            E = n_experts

            gw_in = load(f"gw{layer}", gw[:], ins[f"router{layer}"].rearrange("(k p) n -> p k n", p=P), start)
            gw_ready = split(gw[:], gw_hi[:], gw_lo[:], gw_in, start)

            w_free = Ring(2)
            w_state = {}

            def weight_work(n):
                f0, width, tiles, _ = groups[n]
                cols = width * tiles
                box = {}

                def bring():
                    slot, free = w_free.take()
                    box["slot"], box["free"] = slot, free
                    srcs = {
                        "gate": (stage[:, 0:KB * cols].rearrange("p (k n) -> p k n", k=KB),
                                 ins[f"gate{layer}"][:, f0:f0 + cols].rearrange("(k p) n -> p k n", p=P)),
                        "up": (stage[:, 1024:1024 + KB * cols].rearrange("p (k n) -> p k n", k=KB),
                               ins[f"up{layer}"][:, f0:f0 + cols].rearrange("(k p) n -> p k n", p=P)),
                        "down": (stage[0:width, 2048:2048 + tiles * CH].rearrange("p (k n) -> p k n", k=tiles),
                                 ins[f"down{layer}"][f0:f0 + cols, :].rearrange("(k p) n -> p k n", p=width)),
                    }
                    for dst, src in srcs.values():
                        w_loads[1] += 16
                        sync.quiet(lambda e, dst=dst, src=src: e.dma_start(dst, src).then_inc(w_loads[0], 16),
                                   stage_free[0])
                    box["in"] = (w_loads[0], w_loads[1])

                work = [bring]
                for i, name in enumerate(("gate", "up", "down")):
                    rows = width if name == "down" else P
                    n_cols = tiles * CH if name == "down" else KB * cols

                    def cut(which, i=i, name=name, rows=rows, n_cols=n_cols):
                        src = stage[0:rows, i * 1024:i * 1024 + n_cols]
                        hi, lo = (p[0:rows, box["slot"], 0:n_cols] for p in parts[name])
                        if which == 0:
                            box["t"] = pool(lambda e: copy_on_pool(e, hi, src), box["in"], box["free"], start)
                        else:
                            box["t"] = pool(lambda e: e.tensor_tensor(lo, src, hi.bitcast(F32), ALU.subtract),
                                            box["t"])
                            w_state[n, name] = (box["slot"], box["t"])
                            if name == "down":
                                stage_free[0] = box["t"]

                    work += [lambda c=cut: c(0), lambda c=cut: c(1)]
                return work

            for w in weight_work(0):
                w()

            xt_done = []
            for c in range(4):
                cols = slice(c * 512, (c + 1) * 512)
                xt_done.append(to_channels(lambda i, c=c: x[:, 4 * c + i, :], xt_hi[:, :, cols],
                                           xt_lo[:, :, cols], x_ready[c], start))

            banks = Ring(2)
            for slot in range(2):
                banks.give(slot, *pairs.readers)
            ROUTER_BANKS = (2 * BANK, 5 * BANK)
            logits = buf("logits", [P, ALL_TILES, E])
            logits_t = buf("logits_t", [E, T])

            def logits_known():
                read = [pairs.readers[:], pairs.readers[:]]
                for c in range(4):
                    base = ROUTER_BANKS[c % 2]
                    todo = products(psum[0:E, base:base + 512], [(gw_hi[:, k, :], gw_lo[:, k, :]) for k in range(KB)],
                                    [(xt_hi[:, k, c * 512:(c + 1) * 512], xt_lo[:, k, c * 512:(c + 1) * 512])
                                     for k in range(KB)])
                    for mm in todo[:-1]:
                        pe.quiet(mm, xt_done[c], read[c % 2], gw_ready)
                    lg = pe(todo[-1])
                    read[c % 2] = act(lambda e, c=c, base=base: e.activation(
                        logits_t[:, c * 512:(c + 1) * 512], psum[0:E, base:base + 512], ACT.Copy), lg, start)
                yield
                for t in range(ALL_TILES):
                    base = ROUTER_BANKS[0] + t * E
                    tr = pe(lambda e, t=t, base=base: e.transpose(
                        psum[:, base:base + E], logits_t[:, t * P:(t + 1) * P], ident[0:E, 0:E]), read)
                lg_out = dve(lambda e: e.tensor_copy(
                    logits[:], psum[:, ROUTER_BANKS[0]:ROUTER_BANKS[0] + ALL_TILES * E].rearrange(
                        "p (t n) -> p t n", n=E)), tr, start)
                yield
                return lg_out

            if E == 2:
                top = buf("top", [P, ALL_TILES])
                prob = buf("prob", [P, ALL_TILES, E])
                tot = buf("tot", [P, ALL_TILES])
                is_top = buf("is_top", [P, ALL_TILES, E])
                coef = buf("coef", [P, ALL_TILES, E])
                l0, l1 = logits[:, :, 0], logits[:, :, 1]
                coef_ready = []

                def gating():
                    lg_out = yield from logits_known()
                    r = dve(lambda e: e.tensor_tensor(top[:], l0, l1, ALU.max), lg_out)
                    r = dve(lambda e: e.tensor_tensor(prob[:], logits[:], top[:].unsqueeze(2).to_broadcast(
                        [P, ALL_TILES, E]), ALU.subtract), r)
                    r = act(lambda e: e.activation(prob[:], prob[:], ACT.Exp), r)
                    r = dve(lambda e: e.tensor_tensor(tot[:], prob[:, :, 0], prob[:, :, 1], ALU.add), r)
                    r = dve(lambda e: e.reciprocal(tot[:], tot[:]), r)
                    r = dve(lambda e: e.tensor_tensor(prob[:], prob[:], tot[:].unsqueeze(2).to_broadcast(
                        [P, ALL_TILES, E]), ALU.mult), r)
                    dve(lambda e: e.tensor_tensor(is_top[:, :, 0], prob[:, :, 0], prob[:, :, 1], ALU.is_ge), r)
                    r = dve(lambda e: e.tensor_tensor(is_top[:, :, 1], prob[:, :, 1], prob[:, :, 0], ALU.is_gt), r)
                    coef_ready.append(dve(lambda e: e.tensor_tensor(coef[:], prob[:], is_top[:], ALU.mult), r))
            else:
                TOP_K = 6
                score = buf("score", [P, ALL_TILES, E + 8 - TOP_K])
                best = buf("best", [P, ALL_TILES, 8])
                rest = buf("rest", [P, ALL_TILES, E + 8 - TOP_K])
                tot = buf("tot", [P, ALL_TILES])
                comb = buf("comb", [P, ALL_TILES, E])
                comb_rows = buf("comb_rows", [P, ALL_TILES, P], F32R)
                comb_t = buf("comb_t", [P, T], F32R)
                F = groups[0][0]
                pick_f = buf("pick_f", [P, F], F32R)
                sc = score[:, :, 0:E]
                dve(lambda e: e.memset(score[:], -1.0), start)
                cleared = dve(lambda e: e.memset(comb_rows[:].bitcast(F32), 0.0), start)
                pick_raw = buf("pick_raw", [2 * E, F])
                pick_in = load("pick_f", pick_raw[:], ins["pick_f"], start)
                pick_set = act(lambda e: e.activation(pick_f[0:2 * E, :], pick_raw[:], ACT.Copy), pick_in)
                pick_clear = zero(pick_f[2 * E:P, :], start)

                def gating():
                    lg_out = yield from logits_known()
                    r = act(lambda e: e.activation(logits[:], logits[:], ACT.Exp, scale=-1.0), lg_out)
                    r = dve(lambda e: e.tensor_scalar(logits[:], logits[:], 1.0, None, ALU.add), r)
                    scored = dve(lambda e: e.reciprocal(sc, logits[:]), r)
                    yield
                    for t in range(ALL_TILES):
                        b8 = dve(lambda e, t=t: e.max(best[:, t, :], score[:, t, 0:E]), scored)
                        if t % 8 == 7:
                            yield
                    low = dve(lambda e: e.memset(best[:, :, TOP_K:8], -1.0), b8)
                    for t in range(ALL_TILES):
                        mr = dve(lambda e, t=t: e.match_replace(rest[:, t, :], best[:, t, :], score[:, t, :],
                                                                -2.0), low)
                        if t % 8 == 7:
                            yield
                    r = dve(lambda e: e.tensor_tensor(comb[:], rest[:, :, 0:E], sc, ALU.not_equal), mr)
                    r = dve(lambda e: e.tensor_tensor(comb[:], comb[:], sc, ALU.mult), r)
                    r = dve(lambda e: e.tensor_reduce(tot[:], comb[:], X_AXIS, ALU.add), r)
                    yield
                    r = dve(lambda e: e.tensor_scalar(tot[:], tot[:], 1e-20, None, ALU.add), r)
                    r = dve(lambda e: e.reciprocal(tot[:], tot[:]), r)
                    r = dve(lambda e: e.tensor_tensor(comb[:], comb[:], tot[:].unsqueeze(2).to_broadcast(
                        [P, ALL_TILES, E]), ALU.mult), r)
                    r = dve(lambda e: e.tensor_copy(comb_rows[:, :, 0:E], comb[:]), r, cleared)
                    r = dve(lambda e: e.tensor_tensor(comb_rows[:, :, E:2 * E], comb[:],
                                                      comb_rows[:, :, 0:E].bitcast(F32), ALU.subtract), r)
                    yield
                    free = [banks.readers[0], banks.readers[1]]
                    for c in range(4):
                        bank = (2 + 3 * (c % 2)) * BANK
                        for i in range(4):
                            tr = (lambda e, i=i, c=c, bank=bank: e.transpose(
                                psum[:, bank + i * P:bank + (i + 1) * P],
                                comb_rows[:, 4 * c + i, :].bitcast(F32), ident[:]))
                            if i == 3:
                                turned = pe(tr)
                            else:
                                pe.quiet(tr, r, comb_done[c - 2] if c > 1 else free)
                        comb_done.append(act(lambda e, c=c, bank=bank: e.activation(
                            comb_t[:, c * 512:(c + 1) * 512], psum[:, bank:bank + 512], ACT.Copy), turned))

                comb_done = []

            OUT = 6 * BANK
            out_free = [list(flat(o_read + pairs.readers))]
            bufs = Ring(2)
            pending = []
            work = []
            laid_anew = []

            def down(item):
                n, c, j, slot, hi_ready, lo_ready = item
                f0, width, tiles, kind = groups[n]
                w_slot, w_ready = w_state[n, "down"]
                w_hi, w_lo = (p[0:width, w_slot, j * CH:(j + 1) * CH] for p in parts["down"])
                first, last = j == 0, j == tiles - 1
                for a, w, ready in ((hid_hi, w_hi, hi_ready), (hid_hi, w_lo, hi_ready), (hid_lo, w_hi, lo_ready)):
                    for i in range(4):
                        opens = first and w is w_hi and a is hid_hi and i % 2 == 0
                        closes = last and a is hid_lo
                        mm = (lambda e, a=a, w=w, i=i, opens=opens, closes=closes: e.matmul(
                            psum[:, OUT + i * CH:OUT + (i + 1) * CH], a[0:width, slot, i * P:(i + 1) * P], w,
                            start=opens, stop=closes, skip_group_check=True))
                        if a is hid_lo and i == 3:
                            done = pe(mm)
                        else:
                            pe.quiet(mm, ready, w_ready, out_free[0] if first else None)
                bufs.give(slot, done)
                if last:
                    if c == 3:
                        w_free.give(w_slot, done)
                    xs = x[:, 4 * c:4 * c + 4, :]
                    if kind[0] == "scaled":
                        for i in range(4):
                            t = 4 * c + i
                            added = dve(lambda e, i=i, t=t: e.scalar_tensor_tensor(
                                x[:, t, :], psum[:, OUT + i * CH:OUT + (i + 1) * CH], coef[:, t, kind[1]:kind[1] + 1],
                                x[:, t, :], ALU.mult, ALU.add), done, coef_ready, x_ready[c])
                    else:
                        added = dve(lambda e: e.tensor_tensor(
                            xs.rearrange("p t n -> p (t n)"), psum[:, OUT:OUT + 1024],
                            xs.rearrange("p t n -> p (t n)"), ALU.add), done, x_ready[c])
                    out_free[0] = added
                    x_ready[c] = added
                    if n == len(groups) - 1:
                        laid_anew[:] = fence()
                        x_ready[c] = layernorm(c, added)

            for n, (f0, width, tiles, kind) in enumerate(groups):
                gating_parts = gating() if n == 0 else None
                work += weight_work(n + 1) if n + 1 < len(groups) else []
                for c in range(4):
                    cols = slice(c * 512, (c + 1) * 512)
                    for j in range(tiles):
                        slot, free = banks.take()
                        b_slot, b_free = bufs.take()
                        base = slot * 3 * BANK
                        w_slot = w_state[n, "gate"][0]

                        def weights(name, k):
                            at = k * width * tiles + j * width
                            return tuple(p[:, w_slot, at:at + width] for p in parts[name])

                        rhs = [(xt_hi[:, k, cols], xt_lo[:, k, cols]) for k in range(KB)]
                        done = []
                        for i, name in enumerate(("gate", "up")):
                            todo = products(psum[0:width, base + i * BANK:base + (i + 1) * BANK],
                                            [weights(name, k) for k in range(KB)], rhs)
                            for mm in todo[:-1]:
                                pe.quiet(mm, free, w_state[n, name][1], xt_done[c])
                            done.append(pe(todo[-1]))
                        g_ps, u_ps, c_ps = (psum[0:width, base + i * BANK:base + (i + 1) * BANK] for i in range(3))
                        sg, hd = silu[0:width, b_slot, :], hid[0:width, b_slot, :]
                        hh, hl = hid_hi[0:width, b_slot, :], hid_lo[0:width, b_slot, :]
                        r = act(lambda e, sg=sg, g_ps=g_ps: e.activation(sg, g_ps, ACT.Silu), done[0], b_free, start)
                        if kind[0] == "routed":
                            fs = slice(f0 + j * width, f0 + (j + 1) * width)
                            mix = pe(lambda e, c_ps=c_ps, fs=fs, cols=cols: e.matmul(
                                c_ps, pick_f[:, fs], comb_t[:, cols], start=True, stop=True), comb_done, pick_set, pick_clear)
                            r = dve(lambda e, sg=sg, c_ps=c_ps: e.tensor_tensor(sg, c_ps, sg, ALU.mult), r, mix)
                        r = dve(lambda e, hd=hd, sg=sg, u_ps=u_ps: e.tensor_tensor(hd, u_ps, sg, ALU.mult),
                                r, done[1], b_free)
                        banks.give(slot, r)
                        hi = act(lambda e, hh=hh, hd=hd: e.activation(hh, hd, ACT.Copy), r, b_free)
                        lo = pool(lambda e, hh=hh, hd=hd, hl=hl: e.tensor_tensor(hl, hd, hh.bitcast(F32),
                                                                                 ALU.subtract), hi)
                        while pending:
                            down(pending.pop())
                        if work:
                            work.pop(0)()
                        if gating_parts:
                            next(gating_parts, None)
                        pending.append((n, c, j, b_slot, hi, lo))
                while work:
                    work.pop(0)()
                if gating_parts:
                    for _ in gating_parts:
                        pass
            while pending:
                down(pending.pop())
            pairs.readers[:] = [[(pe.sem, pe.count), (dve.sem, dve.count)]] * 3
            o_read[:] = [[(pe.sem, pe.count), (dve.sem, dve.count)]] * 2
            s.close()
            return laid_anew

        free = attention(0, AttentionShape(16, softmax=False), None)
        free = experts(0, free, [(512 * n, P, 4, ("scaled", n // 2)) for n in range(4)], 2)
        free = attention(1, AttentionShape(32, softmax=True), free)
        experts(1, free, [(3072, 96, 2, ("plain",))] + [(512 * n, P, 4, ("routed",)) for n in range(6)], 32)

        stored = sem("stored")
        for c in range(ALL_TILES // 4):
            sync.quiet(lambda e, c=c: e.dma_start(out_dram[:, 4 * c:4 * c + 4, :],
                                                  x[:, 4 * c:4 * c + 4, :]).then_inc(stored, 16), x_ready[c])

        block = ctx.enter_context(nc.Block())

        @block.sync
        def _(eng):
            sync.play(eng)
            eng.wait_ge(stored, 16 * (ALL_TILES // 4))

        block.tensor(pe.play)
        block.scalar(act.play)
        block.vector(dve.play)
        block.gpsimd(pool.play)


def rope_tables(base_freqs, angles, scale):
    c = np.cos(angles.astype(np.float64))
    s = np.sin(angles.astype(np.float64))
    cos = np.concatenate([c, c], -1)
    sin = np.concatenate([-s, s], -1)
    both = [np.stack([t * scale, t], 1).astype(np.float32) for t in (cos, sin)]
    return [np.ascontiguousarray(t.reshape(TILES, P, 2, -1).transpose(1, 0, 2, 3)) for t in both]


def constants(n_experts, expert_width):
    f32 = np.float32
    d0, d1 = CH // 16, CH // 32
    t = np.arange(SEQ, dtype=f32)
    inv0 = (1.0 / f32(10000.0) ** (np.arange(0, d0, 2, dtype=f32) / f32(d0))).astype(f32)
    cos0, sin0 = rope_tables(inv0, t[:, None] * inv0[None, :], 1.0)
    theta = (f32(10000.0) ** (-np.arange(0, d1, 2, dtype=f32) / f32(d1))).astype(f32)
    temporal = np.floor((np.arange(SEQ) // 72).astype(f32) * 0.5).astype(f32)
    angles = (t[:, None] * theta).astype(np.float64) + (temporal[:, None] * theta).astype(np.float64)
    cos1, sin1 = rope_tables(theta, angles, 1.0 / np.sqrt(d1))
    i = np.arange(P)
    return {
        "ident": np.eye(P, dtype=f32),
        "later": np.stack([np.where(i[None, :] > i[:, None], f32(MASKED), f32(0)),
                           np.where(i[None, :] < i[:, None], f32(MASKED), f32(0))], 1),
        "pick": np.eye(2, dtype=f32),
        "pick_f": np.tile(np.repeat(np.eye(n_experts, dtype=f32), expert_width, axis=1), (2, 1)),
        "cos0": cos0, "sin0": sin0, "cos1": cos1, "sin1": sin1,
    }


def kernel(**inputs):
    import concourse.bacc as bacc
    from concourse.bass_utils import run_bass_kernel_spmd

    a = {k: np.asarray(v) for k, v in inputs.items()}
    width = a["L1_ffn_wd"].shape[0] * a["L1_ffn_wd"].shape[1]

    def by_channel(w):
        return w.transpose(1, 0, 2).reshape(CH, -1)

    arrays = {
        "x": a["L0_attn_x"],
        "wqkv0": a["L0_attn_w_qkv"], "wo0": a["L0_attn_w_out"],
        "ln_scale": a["L0_attn_ln_scale"], "ln_bias": a["L0_attn_ln_bias"],
        "router0": a["L0_ffn_gate_w"].T,
        "gate0": by_channel(a["L0_ffn_w_gate"].transpose(0, 2, 1)),
        "up0": by_channel(a["L0_ffn_w_up"].transpose(0, 2, 1)),
        "down0": a["L0_ffn_w_down"].transpose(0, 2, 1).reshape(-1, CH),
        "wqkv1": np.concatenate([a["L1_attn_Wq"].T, a["L1_attn_Wk"].T, a["L1_attn_Wv"].T], 1),
        "wo1": a["L1_attn_Wo"].T,
        "bias": np.concatenate([a["L1_attn_bq"], a["L1_attn_bk"], a["L1_attn_bv"], a["L1_attn_bo"]]),
        "router1": a["L1_ffn_gate_w"],
        "gate1": np.concatenate([by_channel(a["L1_ffn_wg"]), a["L1_ffn_sg"]], 1),
        "up1": np.concatenate([by_channel(a["L1_ffn_wu"]), a["L1_ffn_su"]], 1),
        "down1": np.concatenate([a["L1_ffn_wd"].reshape(width, CH), a["L1_ffn_sd"]], 0),
        **constants(*a["L1_ffn_wg"].shape[0::2]),
    }
    nc = bacc.Bacc("TRN2", target_bir_lowering=False, num_devices=1)
    feeds, ins = {}, {}
    for name, value in arrays.items():
        value = np.ascontiguousarray(value)
        feeds[f"in_{name}"] = value
        ins[name] = nc.dram_tensor(f"in_{name}", value.shape, mybir.dt.from_np(value.dtype),
                                   kind="ExternalInput").ap()
    out = nc.dram_tensor("out", (BATCH, SEQ, CH), F32, kind="ExternalOutput").ap()
    build_program(nc, ins, out)
    result = run_bass_kernel_spmd(nc, [feeds], core_ids=[0])
    return result.results[0]["out"]
```

```python
from contextlib import ExitStack
from itertools import zip_longest

import numpy as np
import concourse.bass as bass
from concourse import mybir

F32 = mybir.dt.float32
F32R = mybir.dt.float32r
BF16 = mybir.dt.bfloat16
ALU = mybir.AluOpType
ACT = mybir.ActivationFunctionType
X_AXIS = mybir.AxisListType.X
XY_AXES = mybir.AxisListType.XY

P = 128
BATCH, SEQ, CH = 2, 1024, 256
TILES = SEQ // P
HALF = TILES // 2
ALL_TILES = BATCH * TILES
KB = CH // P
BANK = 512
QCH = 512
EPS = 1e-5
WEIGHTS_AHEAD = 2
MASKED = -1e30


class Engine:

    def __init__(self, sem, one_by_one=False):
        self.sem, self.count, self.queue = sem, 0, []
        self.one_by_one = one_by_one

    def __call__(self, issue, *waits):
        if self.one_by_one and self.count:
            waits += ((self.sem, self.count),)
        self.count += 1
        self.queue.append((issue, tuple(flat(waits)), True))
        return (self.sem, self.count)

    def quiet(self, issue, *waits):
        self.queue.append((issue, tuple(flat(waits)), False))

    def mark_last(self):
        issue, waits, signals = self.queue[-1]
        if not signals:
            self.count += 1
            self.queue[-1] = (issue, waits, True)
        return self.count

    def play(self, eng):
        reached = {}
        for issue, waits, signals in self.queue:
            for sem, value in waits:
                if reached.get(sem, 0) < value:
                    eng.wait_ge(sem, value)
                    reached[sem] = value
            inst = issue(eng)
            if signals:
                inst.then_inc(self.sem, 1)


def flat(waits):
    for w in waits:
        if w is None:
            continue
        if isinstance(w, list):
            yield from flat(w)
        else:
            yield w


class Ring:

    def __init__(self, n):
        self.readers, self.at = [None] * n, 0

    def take(self):
        slot = self.at
        self.at = (self.at + 1) % len(self.readers)
        return slot, self.readers[slot]

    def give(self, slot, *tokens):
        self.readers[slot] = list(tokens)


def copy_on_pool(eng, out, in_):
    return eng.tensor_scalar(out, in_, 1.0, 0.0, ALU.mult, ALU.add)


class AttentionShape:

    def __init__(self, heads, softmax):
        self.heads, self.softmax = heads, softmax
        self.d = CH // heads
        self.rows = 32 if softmax else 64
        self.heads_per_group = P // self.rows
        self.groups = heads // self.heads_per_group
        self.quads = heads // 4
        self.groups_per_quad = 4 // self.heads_per_group
        self.v_row = heads * (self.d + 1) + 32


def build_program(nc, ins, out):
    ctx = ExitStack()
    with ctx:
        def sb(name, shape, dt=F32, stack=ctx):
            return stack.enter_context(nc.sbuf_tensor(name, shape, dt))

        def sem(name):
            return ctx.enter_context(nc.semaphore(name))

        pe, act, dve = (Engine(sem(f"{n}_done")) for n in ("pe", "act", "dve"))
        pool = Engine(sem("pool_done"), one_by_one=True)
        sync = Engine(None)

        def load(name, dst, src, *waits):
            s = sem(f"loaded_{name}")
            sync.quiet(lambda e: e.dma_start(dst, src).then_inc(s, 16), *waits)
            return (s, 16)

        def fence():
            return [(e.sem, e.count) for e in (pe, act, dve, pool)]

        psum = ctx.enter_context(nc.psum_tensor("psum", [P, 8 * BANK], F32))
        pairs = Ring(3)
        o_read = [None, None]

        x = sb("x", [P, ALL_TILES, CH])
        stage = sb("stage", [P, 3072])
        ident = sb("ident", [P, P])
        ident_bf = sb("ident_bf", [P, P], BF16)
        later = sb("later", [P, 2, P])
        later_bf = sb("later_bf", [P, 2, P], BF16)
        ln_stats = sb("ln_stats", [P, ALL_TILES, 6])
        ln_mean_var = sb("ln_mean_var", [P, ALL_TILES, 2])
        ln_sd = sb("ln_sd", [P, ALL_TILES])
        ln_rstd = sb("ln_rstd", [P, ALL_TILES])

        x_dram = ins["x"].rearrange("b (t p) c -> p (b t) c", p=P)
        out_dram = out.rearrange("b (t p) c -> p (b t) c", p=P)
        ident_in = load("ident", ident[:], ins["ident"])
        x_ready = [None] * (ALL_TILES // 4)

        def load_x(chunks):
            for c in chunks:
                x_ready[c] = load(f"x{c}", x[:, 4 * c:4 * c + 4, :], x_dram[:, 4 * c:4 * c + 4, :])

        load_x([0])
        later_in = load("later", later[:], ins["later"])
        mask_ready = [dve(lambda e: e.tensor_copy(ident_bf[:], ident[:]), ident_in),
                      dve(lambda e: e.tensor_copy(later_bf[:], later[:]), later_in)]

        def split(src, hi, lo, src_ready, free=None, hurry=False):
            if hurry:
                t = act(lambda e: e.activation(hi, src, ACT.Copy), src_ready, free)
                return dve(lambda e: e.tensor_tensor(lo, src, hi.bitcast(F32), ALU.subtract), t)
            t = pool(lambda e: copy_on_pool(e, hi, src), src_ready, free)
            return pool(lambda e: e.tensor_tensor(lo, src, hi.bitcast(F32), ALU.subtract), t)

        def products(dst, lhs, rhs, last=True, first=True):
            terms = []
            for (lh, ll), (rh, rl) in zip(lhs, rhs):
                terms += [(lh, rh), (lh, rl), (ll, rh)]
            return [(lambda e, a=a, b=b, s=first and i == 0, z=last and i == len(terms) - 1:
                     e.matmul(dst, a, b, start=s, stop=z)) for i, (a, b) in enumerate(terms)]

        def to_channels(src, hi, lo, src_ready, free):
            slot, slot_free = pairs.take()
            bank = psum[:, slot * 1024:(slot + 1) * 1024].rearrange("p (k n) -> p k n", k=KB)
            for k in range(KB):
                for i in range(4):
                    t = (lambda e, k=k, i=i, tile=src(i): e.transpose(
                        bank[:, k, i * P:(i + 1) * P], tile[:, k * P:(k + 1) * P], ident[:]))
                    if (k, i) == (KB - 1, 3):
                        turned = pe(t)
                    else:
                        pe.quiet(t, src_ready, slot_free, ident_in)
            hi_done = act(lambda e: e.activation(hi, bank, ACT.Copy), turned, free)
            lo_done = dve(lambda e: e.tensor_tensor(lo, bank, hi.bitcast(F32), ALU.subtract),
                          hi_done, free)
            pairs.give(slot, lo_done)
            return [hi_done, lo_done]

        def layernorm(c, ready):
            for _ in normalizing(c, ready):
                pass
            return x_ready[c]

        def normalizing(c, ready):
            t0, t1 = 4 * c, 4 * c + 4
            stats = [dve(lambda e, t=t: e.bn_stats(ln_stats[:, t, :], x[:, t, :]), ready)
                     for t in range(t0, t1)]
            for t in range(t0, t1):
                moments = dve(lambda e, t=t: e.bn_aggr(ln_mean_var[:, t, :], ln_stats[:, t, :]), stats[-1])
            sd = dve(lambda e: e.tensor_scalar(ln_sd[:, t0:t1], ln_mean_var[:, t0:t1, 1], EPS, None,
                                               ALU.add), moments)
            yield
            sd = act(lambda e: e.activation(ln_sd[:, t0:t1], ln_sd[:, t0:t1], ACT.Sqrt), sd)
            yield
            rstd = dve(lambda e: e.reciprocal(ln_rstd[:, t0:t1], ln_sd[:, t0:t1]), sd)
            done = [dve(lambda e, t=t: e.tensor_scalar(x[:, t, :], x[:, t, :], ln_mean_var[:, t, 0:1],
                                                       ln_rstd[:, t:t + 1], ALU.subtract, ALU.mult), rstd)
                    for t in range(t0, t1)]
            x_ready[c] = done[-1]

        def zero(dst, *waits):
            rows, n = dst.shape
            return act(lambda e: e.activation(dst, ident[0:rows, 0:1].to_broadcast([rows, n]), ACT.Copy, scale=0.0),
                       ident_in, *waits)

        bias = stage[0:2, 2048:2048 + 4 * CH]
        bias_rows = sb("bias_rows", [2, 4 * CH], F32R)
        pick = sb("pick", [2, 2])
        ones_f = sb("ones_f", [2, P])
        ones = sb("ones", [2, P], F32R)

        def make_bias_rows():
            ready = [load(f"bias{r}", bias[r:r + 1, :], ins["bias"].rearrange("(a n) -> a n", a=1))
                     for r in range(2)]
            ready.append(load("pick", pick[:], ins["pick"]))
            b = pool(lambda e: copy_on_pool(e, bias_rows[:], bias), ready)
            b = pool(lambda e: e.tensor_tensor(bias, bias, bias_rows[:].bitcast(F32), ALU.subtract), b)
            b = pool(lambda e: e.tensor_scalar(bias, bias, pick[:, 1:2], None, ALU.mult), b)
            b = pool(lambda e: e.tensor_scalar(bias_rows[:], bias_rows[:].bitcast(F32), pick[:, 0:1], None,
                                               ALU.mult), b)
            b = pool(lambda e: e.tensor_tensor(bias_rows[:], bias_rows[:].bitcast(F32), bias, ALU.add), b)
            o = pool(lambda e: e.memset(ones_f[:], 1.0), b)
            return pool(lambda e: copy_on_pool(e, ones[:], ones_f[:]), o)

        stage_free, bias_ready = [None], []

        def attention(layer, shape, start):
            s = ExitStack()
            H, d, R = shape.heads, shape.d, shape.rows
            HG = shape.heads_per_group

            def buf(name, sh, dt=F32):
                return sb(f"{name}{layer}", sh, dt, s)

            w_hi = buf("wqkv_hi", [P, KB, 3 * CH], F32R)
            w_lo = buf("wqkv_lo", [P, KB, 3 * CH], F32R)
            wo_hi = buf("wo_hi", [P, KB, CH], F32R)
            wo_lo = buf("wo_lo", [P, KB, CH], F32R)
            cos = buf("cos", [P, TILES, 2, d])
            sin = buf("sin", [P, TILES, 2, d])
            qk = buf("qk", [P, TILES, 2, CH])
            v = buf("v", [P, TILES, shape.v_row])
            xt = buf("xt", [P, 2 * KB * SEQ], F32R)
            xt_hi = xt[:, 0:KB * SEQ].rearrange("p (k n) -> p k n", k=KB)
            xt_lo = xt[:, KB * SEQ:].rearrange("p (k n) -> p k n", k=KB)
            q_rows = buf("q_rows", [P, 2, TILES * P], F32R)
            k_rows = buf("k_rows", [P, 1, TILES * P], F32R)
            qt = buf("qt", [P, 4, SEQ], F32R)
            kt = buf("kt", [P, SEQ])
            km = buf("km", [P, 2, 4, SEQ], F32R)
            probs = buf("probs", [P, WEIGHTS_AHEAD + 2, 4, QCH])
            o_cols = buf("o_cols", [P, 2, SEQ])
            ao = buf("ao", [P, TILES, CH])
            o_rcp = buf("o_rcp", [P, 2, TILES, 4])

            ROTATING = 6

            def rotated(u, which):
                return probs[:, u // 2, 2 * (u % 2) + which, :]

            def masked_k(slot):
                return km[:, slot] if slot < 2 else xt[:, :].rearrange("p (h n) -> p h n", h=4)

            def pieces(rows, slot):
                return rows[:, slot, :].rearrange("p (t h f) -> p t h f", t=TILES, h=HG)

            w_in = load(f"wqkv{layer}", stage[:, 0:KB * 3 * CH].rearrange("p (k n) -> p k n", k=KB),
                        ins[f"wqkv{layer}"].rearrange("(k p) n -> p k n", p=P), stage_free[0])
            wo_in = load(f"wo{layer}", stage[:, KB * 3 * CH:KB * 4 * CH].rearrange("p (k n) -> p k n", k=KB),
                         ins[f"wo{layer}"].rearrange("(k p) n -> p k n", p=P), stage_free[0])
            if start is None:
                load_x([1])
            cos_in = load(f"cos{layer}", cos[:], ins[f"cos{layer}"], start)
            sin_in = load(f"sin{layer}", sin[:], ins[f"sin{layer}"], start)
            w_ready = split(stage[:, 0:KB * 3 * CH], w_hi[:, :, :].rearrange("p k n -> p (k n)"),
                            w_lo[:, :, :].rearrange("p k n -> p (k n)"), w_in, start, hurry=True)
            v_ones = pool(lambda e: e.memset(v[:], 1.0), start)
            rows_clear = [pool(lambda e: e.memset(q_rows[:].bitcast(F32), 0.0), start),
                          pool(lambda e: e.memset(k_rows[:].bitcast(F32), 0.0), start)]
            if shape.softmax:
                rows_clear.append(dve(lambda e: e.memset(
                    pieces(k_rows, 0)[:, :, :, 3 * d:3 * d + 2].bitcast(F32), 1.0), rows_clear[1]))
                neg_max = buf("neg_max", [P, 2, 2, TILES, 4])
                no_keys_before = dve(lambda e: e.memset(neg_max[:, :, 1, 0, :], -MASKED), start)
            else:
                qk_scale = buf("qk_scale", [P, d])
                qk_bias = buf("qk_bias", [P, d])
                scale_in = load("qk_scale", qk_scale[:], ins["ln_scale"].partition_broadcast(P), start)
                shift_in = load("qk_bias", qk_bias[:], ins["ln_bias"].partition_broadcast(P), start)
                mom = o_cols[:, 1, 0:ROTATING * 8 * H].rearrange("p (u m g) -> p u m g", u=ROTATING, m=4)

            wo_ready = split(stage[:, KB * 3 * CH:KB * 4 * CH], wo_hi[:, :, :].rearrange("p k n -> p (k n)"),
                             wo_lo[:, :, :].rearrange("p k n -> p (k n)"), wo_in, start)
            stage_free[0] = wo_ready
            if start is None:
                load_x([2, 3])
                bias_ready.append(make_bias_rows())
                stage_free[0] = [wo_ready, bias_ready[0]]

            q_taken = Ring(2)
            k_read, kt_read = [None, None], [None, None]
            qt_taken = Ring(4) if not shape.softmax else (Ring(2), Ring(2))
            km_taken = Ring(3 if shape.softmax else 2)
            p_taken = Ring(WEIGHTS_AHEAD + 2)
            oc_taken = Ring(2)

            def x_to_channels(b, c, free):
                cols = slice(c * 512, (c + 1) * 512)
                return to_channels(lambda i: x[:, b * TILES + 4 * c + i, :], xt_hi[:, :, cols], xt_lo[:, :, cols],
                                   x_ready[2 * b + c], free)

            norms_due = []

            def norm():
                g = norms_due.pop(0)
                x_ready[g] = layernorm(g, x_ready[g])

            for b in range(BATCH):
                before = before_next if b else start
                km_taken.at = 0

                xt_done = [x_to_channels(b, 0, before) if b == 0 else first_chunk, x_to_channels(b, 1, before)]
                v_done, qk_done = [], [None] * TILES
                chain = {}

                def project(t):
                    slot, slot_free = pairs.take()
                    base = slot * 1024
                    cols = slice(t * P, (t + 1) * P)
                    first = True
                    for k in range(KB):
                        for a, w in ((xt_hi, w_hi), (xt_hi, w_lo), (xt_lo, w_hi)):
                            end = k == KB - 1 and a is xt_lo and not shape.softmax
                            pe.quiet(lambda e, a=a, w=w, k=k, f=first, z=end: e.matmul(
                                psum[:, base:base + 512], a[:, k, cols], w[:, k, 0:512], start=f, stop=z),
                                xt_done[t // 4], slot_free, w_ready)
                            mm = (lambda e, a=a, w=w, k=k, f=first, z=end: e.matmul(
                                psum[:, base + 512:base + 768], a[:, k, cols], w[:, k, 512:768], start=f, stop=z))
                            first = False
                            if end:
                                projected = pe(mm)
                            else:
                                pe.quiet(mm)
                    if shape.softmax:
                        pe.quiet(lambda e: e.matmul(psum[:, base:base + 512], ones[:], bias_rows[:, 0:512],
                                                    start=False, stop=True), bias_ready)
                        projected = pe(lambda e: e.matmul(psum[:, base + 512:base + 768], ones[:],
                                                          bias_rows[:, 512:768], start=False, stop=True))
                    vv = v[:, t, 0:H * (d + 1)].rearrange("p (h e) -> p h e", h=H)[:, :, 0:d]
                    v_out = act(lambda e: e.activation(
                        vv, psum[:, base + 512:base + 768].rearrange("p (h e) -> p h e", h=H), ACT.Copy),
                        projected, v_ones, before)
                    v_done.append(v_out)

                    u = t % ROTATING
                    pq = psum[:, base:base + 512].rearrange("p (s h e) -> p s h e", s=2, h=H)
                    ra = rotated(u, 0).rearrange("p (s h e) -> p s h e", s=2, h=H)
                    rb = rotated(u, 1).rearrange("p (s h e) -> p s h e", s=2, h=H)
                    h2 = d // 2

                    def table(tb, lo, hi):
                        return tb[:, t, :, lo:hi].unsqueeze(2).to_broadcast([P, 2, H, hi - lo])

                    free = [before, chain.get(("free", u))]
                    dve(lambda e: e.tensor_tensor(ra, pq, table(cos, 0, d), ALU.mult), projected, cos_in, free)
                    dve(lambda e: e.tensor_tensor(rb[:, :, :, 0:h2], pq[:, :, :, h2:d], table(sin, 0, h2),
                                                  ALU.mult), sin_in)
                    b2 = dve(lambda e: e.tensor_tensor(rb[:, :, :, h2:d], pq[:, :, :, 0:h2],
                                                       table(sin, h2, d), ALU.mult))
                    pairs.give(slot, v_out, b2)
                    if shape.softmax:
                        done = dve(lambda e: e.tensor_tensor(qk[:, t].rearrange("p s (h e) -> p s h e", h=H),
                                                             ra, rb, ALU.add), b2)
                        qk_done[t] = done
                        chain["free", u] = done
                        return
                    yield
                    ra2 = rotated(u, 0).rearrange("p (g e) -> p g e", e=d)
                    rb2 = rotated(u, 1).rearrange("p (g e) -> p g e", e=d)
                    m = mom[:, u]
                    r = dve(lambda e: e.tensor_tensor(rotated(u, 0), rotated(u, 0), rotated(u, 1), ALU.add), b2)
                    yield
                    r = dve(lambda e: e.tensor_reduce(m[:, 0], ra2, X_AXIS, ALU.add), r)
                    yield
                    r = dve(lambda e: e.scalar_tensor_tensor(ra2, m[:, 0].unsqueeze(2).to_broadcast([P, 2 * H, d]),
                                                             -1.0 / d, ra2, ALU.mult, ALU.add), r)
                    chain["sq", t] = act(lambda e: e.activation(rb2, ra2, ACT.Square), r)

                def spread(t):
                    u = t % ROTATING
                    m = mom[:, u]
                    rb2 = rotated(u, 1).rearrange("p (g e) -> p g e", e=d)
                    r = dve(lambda e: e.tensor_reduce(m[:, 1], rb2, X_AXIS, ALU.add), chain["sq", t])
                    yield
                    r = dve(lambda e: e.tensor_scalar(m[:, 1], m[:, 1], 1.0 / d, EPS, ALU.mult, ALU.add), r)
                    chain["sd", t] = act(lambda e: e.activation(m[:, 2], m[:, 1], ACT.Sqrt), r)

                def scale(t):
                    u = t % ROTATING
                    m = mom[:, u]
                    ra2 = rotated(u, 0).rearrange("p (g e) -> p g e", e=d)
                    yield
                    r = dve(lambda e: e.reciprocal(m[:, 3], m[:, 2]), chain["sd", t])
                    where = dve if t >= TILES - 2 else pool
                    r = where(lambda e: e.tensor_tensor(ra2, ra2, m[:, 3].unsqueeze(2).to_broadcast([P, 2 * H, d]),
                                                        ALU.mult), r)
                    r = where(lambda e: e.tensor_tensor(ra2, ra2, qk_scale[:].unsqueeze(1).to_broadcast([P, 2 * H, d]),
                                                        ALU.mult), r, scale_in)
                    done = where(lambda e: e.tensor_tensor(
                        qk[:, t].rearrange("p s (h e) -> p (s h) e", h=H), ra2,
                        qk_bias[:].unsqueeze(1).to_broadcast([P, 2 * H, d]), ALU.add), r, shift_in, before)
                    qk_done[t] = done
                    chain["free", u] = done

                group_ready, qt_ready, km_ready = {}, {}, {}

                def cut_pieces(g, t0=0, t1=TILES, hurry=False):
                    for _ in cutting(g, t0, t1, hurry):
                        pass

                def cutting(g, t0=0, t1=TILES, hurry=False):
                    if t0 == 0:
                        group_ready[g] = [*q_taken.take(), None]
                    slot, free = group_ready[g][0:2]
                    hd = slice(g * HG * d, (g + 1) * HG * d)

                    def src(which):
                        return qk[:, t0:t1, which, hd].rearrange("p t (h e) -> p t h e", h=HG)

                    def put(rows, at):
                        return pieces(rows, slot if rows is q_rows else 0)[:, t0:t1, :, at * d:(at + 1) * d]

                    def copy(dst, src, *waits):
                        if hurry:
                            return act(lambda e: e.activation(dst, src, ACT.Copy), *waits)
                        return pool(lambda e: copy_on_pool(e, dst, src), *waits)

                    hi_at = ((0, 1), (0, 2))
                    lo_at = ((2,), (1,)) if shape.softmax else ((2, 3), (1, 3))
                    waits = [qk_done[t0:t1], rows_clear, free, k_read[t0 // 4:t1 // 4]]
                    done = []
                    for which, rows in ((0, q_rows), (1, k_rows)):
                        hi = copy(put(rows, hi_at[which][0]), src(which), waits)
                        low = (dve if hurry else pool)(lambda e, w=which, r=rows: e.tensor_tensor(
                            put(r, lo_at[w][0]), src(w), put(r, hi_at[w][0]).bitcast(F32), ALU.subtract),
                            hi, waits)
                        yield
                        hi = copy(put(rows, hi_at[which][1]), src(which), waits)
                        last = [hi, low]
                        if not shape.softmax:
                            last.append(copy(put(rows, 3), put(rows, lo_at[which][0]).bitcast(F32), low))
                        elif which == 0:
                            last.append((dve if hurry else pool)(lambda e: e.memset(
                                pieces(q_rows, slot)[:, t0:t1, :, 3 * d:3 * d + 2].bitcast(F32), 0.0), waits))
                        done.append(last)
                        if which == 0:
                            yield
                    group_ready[g][2] = done

                def turn_pieces(g, t0=0, t1=TILES):
                    slot, _, done = group_ready[g]
                    cols = slice(t0 * P, t1 * P)

                    def turn(rows, at, ready):
                        pair, pair_free = pairs.take()
                        for t in range(t0, t1):
                            tr = (lambda e, t=t: e.transpose(
                                psum[:, pair * 1024 + (t - t0) * P:pair * 1024 + (t - t0 + 1) * P],
                                rows[:, at, t * P:(t + 1) * P].bitcast(F32), ident[:]))
                            if t == t1 - 1:
                                turned = pe(tr)
                            else:
                                pe.quiet(tr, ready, pair_free)
                        return pair, psum[:, pair * 1024:pair * 1024 + (t1 - t0) * P], turned

                    if t0 == 0:
                        q_slot, q_free = (qt_taken[0] if shape.softmax else qt_taken).take()
                        qt_ready[g] = (q_slot, [q_free])
                    q_slot, q_ready = qt_ready[g]
                    pair, at, turned = turn(q_rows, slot, done[0])
                    q_out = act(lambda e, at=at: e.activation(qt[:, q_slot, cols], at, ACT.Copy),
                                turned, q_ready[0], before)
                    pairs.give(pair, q_out)
                    q_ready.append(q_out)
                    pair, at, turned = turn(k_rows, 0, done[1])
                    for half in range(t0 // 4, t1 // 4):
                        k_read[half] = turned
                    if not shape.softmax and t1 == TILES:
                        q_taken.give(slot, turned)
                    k_out = act(lambda e, at=at: e.activation(kt[:, cols], at, ACT.Copy),
                                turned, kt_read[t0 // 4:t1 // 4], before)
                    pairs.give(pair, k_out)
                    quad, part = divmod(g, shape.groups_per_quad)
                    if part == 0 and t0 == 0:
                        m_slot, m_free = km_taken.take()
                        km_ready[quad] = [m_slot, m_free]
                    m_slot, m_free = km_ready[quad][0:2]
                    for h in range(HG):
                        r = slice(h * R, (h + 1) * R)
                        m_out = pool(lambda e, h=h, r=r: copy_on_pool(
                            e, masked_k(m_slot)[r, part * HG + h, cols], kt[r, cols]), k_out, m_free, rows_clear)
                    km_ready[quad].append(m_out)
                    for half in range(t0 // 4, t1 // 4):
                        kt_read[half] = m_out

                max_done = {}

                def max_units(t0=0, t1=TILES):
                    units = []
                    for i in range(t0, t1):
                        if i % 2 == 0:
                            units.append((i, None, None))
                        w = i * P
                        per = 4 if w <= 256 else 2 if w <= 512 else 1
                        units += [(i, h0, per) for h0 in range(0, 4, per) if w]
                    return units

                def max_unit(g, unit):
                    i, h0, n = unit
                    slot, slot_free = pairs.take()
                    base = slot * 1024
                    q_slot, q_ready = qt_ready[g]
                    keys = masked_k(km_ready[g][0])
                    waits = [slot_free, q_ready, km_ready[g][2:], mask_ready, max_done.get(("cut", g - 2))]

                    def score(tile, at, heads, k0, k1, masked=False):
                        dst = psum[:, at:at + (k1 - k0) * len(heads)].rearrange("p (h n) -> p h n", h=len(heads))
                        pe.quiet(lambda e: e.matmul(dst, qt[:, q_slot, tile * P:(tile + 1) * P],
                                                    keys[:, heads[0]:heads[-1] + 1, k0:k1],
                                                    start=True, stop=not masked), waits)

                    if h0 is None:
                        for u in range(2):
                            tile, at = i + u, base + u * 512
                            score(tile, at, range(4), tile * P, (tile + 1) * P, masked=True)
                            scored = pe(lambda e, at=at: e.matmul(
                                psum[:, at:at + 512].rearrange("p (h n) -> p h n", h=4), ident_bf[:],
                                later_bf[:, 0, :].unsqueeze(1).to_broadcast([P, 4, P]), start=False, stop=True))
                        view = psum[:, base:base + 1024].rearrange("p (t h n) -> p t h n", t=2, h=4)
                        m = dve(lambda e: e.tensor_reduce(neg_max[:, g % 2, 0, i:i + 2, :], view, X_AXIS, ALU.max,
                                                          negate=True), scored, before)
                    else:
                        w = i * P
                        per, part, stride = (512 // w, w, w) if w <= 256 else (1, w, 512) if w <= 512 else (1, w // 2, 512)
                        halves = w // part
                        for h in range(h0, h0 + n, per):
                            for k0 in range(0, w, part):
                                score(i, base + ((h - h0) * halves + k0 // part) * stride, range(h, h + per),
                                      k0, k0 + part)
                        scored = (pe.sem, pe.mark_last())
                        view = psum[:, base:base + n * halves * stride].rearrange(
                            "p (h s n) -> p h s n", h=n, s=halves)[:, :, :, 0:part]
                        m = dve(lambda e: e.tensor_reduce(neg_max[:, g % 2, 1, i, h0:h0 + n], view, XY_AXES, ALU.max,
                                                          negate=True), scored, before)
                    pairs.give(slot, m)
                    if i == TILES - 1 and h0 == 3:
                        qt_taken[0].give(q_slot, scored)
                    max_done[g] = m

                def cut_max(g, half):
                    slot = group_ready[g][0]
                    t0, t1 = half * 4, half * 4 + 4
                    nm = neg_max[:, g % 2, 0, t0:t1, :]
                    m = dve(lambda e: e.tensor_tensor(nm, nm, neg_max[:, g % 2, 1, t0:t1, :], ALU.min),
                            max_done[g], no_keys_before)
                    nm = nm.unsqueeze(3)
                    at = pieces(q_rows, slot)[:, t0:t1, :, 3 * d:3 * d + 1]
                    at_lo = pieces(q_rows, slot)[:, t0:t1, :, 3 * d + 1:3 * d + 2]
                    m = pool(lambda e: copy_on_pool(e, at, nm), m)
                    m = pool(lambda e: e.tensor_tensor(at_lo, nm, at.bitcast(F32), ALU.subtract), m)
                    max_done["cut", g] = max_done["cut", g, half] = m

                def turn_max(g, half):
                    slot, m = group_ready[g][0], max_done["cut", g, half]
                    t0, t1 = half * 4, half * 4 + 4
                    pair, pair_free = pairs.take()
                    for t in range(t0, t1):
                        tr = (lambda e, t=t: e.transpose(
                            psum[:, pair * 1024 + (t - t0) * P:pair * 1024 + (t - t0 + 1) * P],
                            q_rows[:, slot, t * P:(t + 1) * P].bitcast(F32), ident[:]))
                        if t == t1 - 1:
                            turned = pe(tr)
                        else:
                            pe.quiet(tr, m, pair_free)
                    if half:
                        q_taken.give(slot, turned)
                    if half == 0:
                        q_slot, q_free = qt_taken[1].take()
                        qt_ready["max", g] = [q_slot, q_free]
                    q_slot, q_free = qt_ready["max", g][0:2]
                    q_out = act(lambda e: e.activation(qt[:, 2 + q_slot, half * 512:(half + 1) * 512],
                                                       psum[:, pair * 1024:pair * 1024 + 512], ACT.Copy),
                                turned, q_free, before)
                    pairs.give(pair, q_out)
                    qt_ready["max", g].append(q_out)

                weighed = []
                o_turn = {}

                def weigh(step):
                    quad, c, key, q0, w, slot, ready = step
                    bank = (6 + c) * BANK
                    bank_free = o_read[c] if key == 0 else None
                    for h in range(4):
                        at = (4 * quad + h) * (d + 1)
                        mm = (lambda e, h=h, at=at: e.matmul(
                            psum[32 * h:32 * h + 32, bank + q0:bank + QCH], v[:, key, at:at + 32],
                            probs[:, slot, h, 0:w], start=(key == 0), stop=(key == 4 * c + 3)))
                        if h == 3:
                            done = pe(mm)
                        else:
                            pe.quiet(mm, ready, bank_free, v_done)
                    p_taken.give(slot, done)
                    if key == 4 * c + 3:
                        if c == 0:
                            o_turn[quad] = list(oc_taken.take())
                        oc, oc_free = o_turn[quad][0:2]
                        o_out = act(lambda e: e.activation(o_cols[:, oc, c * QCH:(c + 1) * QCH],
                                                           psum[:, bank:bank + QCH], ACT.Copy), done, oc_free)
                        o_turn[quad].append(o_out)
                        o_read[c] = o_out

                def weights_step(quad, c, key):
                    j = key - 4 * c
                    q0 = max(j, 0) * P
                    w = QCH - q0
                    per = 2 if w > 256 else 4
                    keys = masked_k(km_ready[quad][0])
                    masks = j >= 0 and shape.softmax
                    p_slot, p_free = p_taken.take()
                    ready = []
                    for h0 in range(0, 4, per):
                        slot, slot_free = pairs.take()
                        base = slot * 1024
                        early = max(0, 256 - w)
                        stride = 512 if per == 2 else w + early
                        in_bank = 512 // stride
                        for h in range(h0, h0 + per):
                            if shape.softmax:
                                q_slot, q_ready = 2 + qt_ready["max", quad][0], qt_ready["max", quad][2 + c]
                            else:
                                q_slot, q_ready = qt_ready[2 * quad + h // 2]
                            at = base + (h - h0) * stride
                            opens = not masks or h % in_bank == 0
                            mm = (lambda e, h=h, at=at, q_slot=q_slot, opens=opens: e.matmul(
                                psum[:, at:at + early + w], keys[:, h, key * P:(key + 1) * P],
                                qt[:, q_slot, c * QCH + q0 - early:(c + 1) * QCH],
                                start=opens, stop=not masks, skip_group_check=masks))
                            if masks:
                                pe.quiet(mm, slot_free, q_ready, km_ready[quad][2:])
                                if (h + 1) % in_bank:
                                    continue
                                at -= (in_bank - 1) * stride
                                mm = (lambda e, at=at, n=in_bank, early=early, stride=stride: e.matmul(
                                    psum[:, at:at + n * stride].rearrange("p (h n) -> p h n", h=n)[:, :, early:early + P],
                                    ident_bf[:], later_bf[:, 1, :].unsqueeze(1).to_broadcast([P, n, P]),
                                    start=False, stop=True, skip_group_check=True))
                            if h == h0 + per - 1:
                                scored = pe(mm, q_ready)
                            else:
                                pe.quiet(mm, slot_free, q_ready, km_ready[quad][2:])
                        view = psum[:, base:base + per * stride].rearrange("p (h n) -> p h n", h=per)[
                            :, :, early:early + w]
                        dst = probs[:, p_slot, h0:h0 + per, 0:w]
                        t = act(lambda e, view=view, dst=dst: e.activation(
                            dst, view, ACT.Exp if shape.softmax else ACT.Square), scored, p_free, qk_done)
                        pairs.give(slot, t)
                        if not shape.softmax:
                            where = pool if key == 3 and h0 == 0 and j < 0 else dve
                            t = where(lambda e, dst=dst: e.tensor_tensor(dst, dst, dst, ALU.mult), t)
                        ready.append(t)
                        if h0 == 0:
                            yield
                    if j >= 0 and not shape.softmax:
                        dst = probs[:, p_slot, :, 0:P]
                        ready.append(pool(lambda e: e.affine_select(
                            out=dst, in_=dst, compare_op=ALU.is_ge, fill=0.0, base=0,
                            pattern=[[0, 4], [1, P]], channel_multiplier=-1), ready[:]))
                    if key == 4 * c + 3 and c == 1:
                        km_taken.give(km_ready[quad][0], scored)
                        if shape.softmax:
                            qt_taken[1].give(qt_ready["max", quad][0], scored)
                        else:
                            for g in (2 * quad, 2 * quad + 1):
                                qt_taken.give(qt_ready[g][0], scored)
                    weighed.append((quad, c, key, q0, w, p_slot, ready))
                    if len(weighed) > WEIGHTS_AHEAD:
                        weigh(weighed.pop(0))

                def normalize(quad, t0=0, t1=TILES):
                    while weighed and weighed[0][0] == quad and weighed[0][1] * 4 < t1:
                        weigh(weighed.pop(0))
                    oc = o_turn[quad][0]
                    pair, pair_free = pairs.take()
                    for t in range(t0, t1):
                        tr = (lambda e, t=t: e.transpose(
                            psum[:, pair * 1024 + (t - t0) * P:pair * 1024 + (t - t0 + 1) * P],
                            o_cols[:, oc, t * P:(t + 1) * P], ident[:]))
                        if t == t1 - 1:
                            turned = pe(tr)
                        else:
                            pe.quiet(tr, o_turn[quad][2:], pair_free)
                    if t1 == TILES:
                        oc_taken.give(oc, turned)
                    o = psum[:, pair * 1024:pair * 1024 + (t1 - t0) * P].rearrange("p (t h e) -> p t h e", t=t1 - t0, h=4)
                    rcp = o_rcp[:, quad % 2, t0:t1].unsqueeze(3)
                    r = dve(lambda e: e.reciprocal(rcp, o[:, :, :, d:d + 1]), turned, before)
                    dst = ao[:, t0:t1, quad * 4 * d:(quad + 1) * 4 * d].rearrange("p t (h e) -> p t h e", h=4)
                    done = dve(lambda e: e.tensor_tensor(
                        dst, o[:, :, :, 0:d], rcp.to_broadcast([P, t1 - t0, 4, d]), ALU.mult), r)
                    pairs.give(pair, done)
                    return done

                turned_out = {}

                def turn_out(c, ready):
                    cols = slice(c * 512, (c + 1) * 512)
                    turned_out[c] = to_channels(lambda i: ao[:, 4 * c + i, :], xt_hi[:, :, cols], xt_lo[:, :, cols],
                                                ready, (pe.sem, pe.count))

                def project_out(c):
                    slot, slot_free = pairs.take()
                    base = slot * 1024
                    for i in range(4):
                        dst = psum[:, base + i * CH:base + (i + 1) * CH]
                        tk = slice((4 * c + i) * P, (4 * c + i + 1) * P)
                        todo = products(dst, [(xt_hi[:, k, tk], xt_lo[:, k, tk]) for k in range(KB)],
                                        [(wo_hi[:, k, :], wo_lo[:, k, :]) for k in range(KB)],
                                        last=not shape.softmax)
                        if shape.softmax:
                            todo.append(lambda e, dst=dst: e.matmul(dst, ones[:], bias_rows[:, 3 * CH:4 * CH],
                                                                    start=False, stop=True))
                        for mm in todo[:-1]:
                            pe.quiet(mm, turned_out[c], slot_free, wo_ready)
                        projected = pe(todo[-1])
                    g = 2 * b + c
                    xs = x[:, 4 * g:4 * g + 4, :].rearrange("p t n -> p (t n)")
                    added = dve(lambda e: e.tensor_tensor(xs, psum[:, base:base + 1024], xs, ALU.add),
                                projected, x_ready[g])
                    pairs.give(slot, added)
                    x_ready[g] = added
                    norms_due.append(g)

                def first_max(i0, i1):
                    for unit in max_units(i0, i1):
                        max_unit(0, unit)

                for t in range(TILES + 2):
                    parts = [project(t)] if t < TILES else []
                    if not shape.softmax:
                        parts += [spread(t - 1)] if 1 <= t <= TILES else []
                        parts += [scale(t - 2)] if 2 <= t else []
                    for _ in zip_longest(*parts):
                        pass
                    if b == 0 and 1 <= t < TILES:
                        for n in (t - 1,) if t < TILES - 1 else (t - 1, t):
                            rows_clear.append(zero(km[:, n // 4, n % 4, :], start))
                    if not shape.softmax and t == HALF + 3:
                        for g in (0, 1):
                            cut_pieces(g, 0, HALF, hurry=True)
                            turn_pieces(g, 0, HALF)
                    if shape.softmax and t == HALF + 1:
                        cut_pieces(0, 0, HALF, hurry=True)
                        turn_pieces(0, 0, HALF)
                    if shape.softmax and HALF + 1 < t < TILES:
                        first_max(2 * (t - HALF - 2), 2 * (t - HALF - 1))
                projected_all = (pe.sem, pe.count)
                if shape.softmax:
                    cut_pieces(0, HALF, TILES, hurry=True)
                    turn_pieces(0, HALF, TILES)
                    km_taken.give(2, [zero(masked_k(2)[:, h, :], projected_all) for h in range(4)])
                    cut_max(0, 0)
                    cut_pieces(1)
                    turn_max(0, 0)
                else:
                    for g in (0, 1):
                        cut_pieces(g, HALF, TILES, hurry=True)
                        turn_pieces(g, HALF, TILES)
                for quad in range(shape.quads):
                    steps = [(c, key) for c in range(SEQ // QCH) for key in range(4 * c + 4)]
                    between = [(5, norm)] if norms_due and quad < 2 else []
                    if quad:
                        between.append((3, lambda q=quad - 1: normalize(q)))
                    if shape.softmax:
                        begin = 0 if quad else 3.5
                        if not quad:
                            units = max_units(HALF)
                            for n, unit in enumerate(units):
                                between.append((n * begin / len(units), lambda unit=unit: max_unit(0, unit)))
                            between.append((2, lambda: turn_pieces(1)))
                        between.append((begin, lambda q=quad: cut_max(q, 1)))
                        between.append((begin + (3 if quad else 0.5), lambda q=quad: turn_max(q, 1)))
                        if quad + 2 < shape.quads:
                            between.append((4, lambda q=quad + 2: cut_pieces(q)))
                            between.append((9, lambda q=quad + 2: turn_pieces(q)))
                        if quad + 1 < shape.quads:
                            units = max_units()
                            for n, unit in enumerate(units):
                                between.append((0.25 + begin + n * (11.5 - begin) / len(units),
                                                lambda q=quad + 1, unit=unit: max_unit(q, unit)))
                            between.append((7 if quad else 9, lambda q=quad + 1: cut_max(q, 0)))
                            between.append((10 if quad else 11, lambda q=quad + 1: turn_max(q, 0)))
                    elif quad + 1 < shape.quads:
                        for g, at in ((2 * quad + 2, 0), (2 * quad + 3, 4)):
                            parts = cutting(g)
                            for n in range(4):
                                between.append((at + n, lambda parts=parts: next(parts, None)))
                            between.append((at + 4.5, lambda g=g: turn_pieces(g)))
                    if quad == shape.quads - 1:
                        between.append((7, lambda q=quad: turned_out.update(ready=normalize(q, 0, HALF))))
                        between.append((9, lambda: turn_out(0, turned_out["ready"])))
                        between.append((11, lambda: project_out(0)))
                    between.sort(key=lambda p: p[0])
                    for n, (c, key) in enumerate(steps):
                        half_steps = weights_step(quad, c, key)
                        for at in (n, n + 0.5) if shape.softmax else (n, n):
                            while between and between[0][0] <= at:
                                between.pop(0)[1]()
                            next(half_steps, None)
                    for _, what in between:
                        what()
                while weighed:
                    weigh(weighed.pop(0))
                before_next = fence()
                turn_out(1, normalize(shape.quads - 1, HALF, TILES))
                if b + 1 < BATCH:
                    first_chunk = x_to_channels(b + 1, 0, (pe.sem, pe.count))
                project_out(1)
                before_next += fence()
            laid_anew = fence()
            while norms_due:
                norm()
            s.close()
            return laid_anew

        w_loads = [sem("loaded_weights"), 0]

        def experts(layer, start, groups, n_experts):
            s = ExitStack()

            def buf(name, sh, dt=F32):
                return sb(f"{name}{layer}", sh, dt, s)

            T = BATCH * SEQ
            xt_hi = buf("fxt_hi", [P, KB, T], F32R)
            xt_lo = buf("fxt_lo", [P, KB, T], F32R)
            parts = {n: (buf(f"{n}_hi", [P, 2, 1024], F32R), buf(f"{n}_lo", [P, 2, 1024], F32R))
                     for n in ("gate", "up", "down")}
            silu = buf("silu", [P, 2, 512])
            hid = buf("hid", [P, 2, 512])
            hid_hi = buf("hid_hi", [P, 2, 512], F32R)
            hid_lo = buf("hid_lo", [P, 2, 512], F32R)
            gw = buf("gw", [P, KB, n_experts])
            gw_hi = buf("gw_hi", [P, KB, n_experts], F32R)
            gw_lo = buf("gw_lo", [P, KB, n_experts], F32R)
            E = n_experts

            gw_in = load(f"gw{layer}", gw[:], ins[f"router{layer}"].rearrange("(k p) n -> p k n", p=P), start)
            gw_ready = split(gw[:], gw_hi[:], gw_lo[:], gw_in, start)

            w_free = Ring(2)
            w_state = {}

            def weight_work(n):
                f0, width, tiles, _ = groups[n]
                cols = width * tiles
                box = {}

                def bring():
                    slot, free = w_free.take()
                    box["slot"], box["free"] = slot, free
                    srcs = {
                        "gate": (stage[:, 0:KB * cols].rearrange("p (k n) -> p k n", k=KB),
                                 ins[f"gate{layer}"][:, f0:f0 + cols].rearrange("(k p) n -> p k n", p=P)),
                        "up": (stage[:, 1024:1024 + KB * cols].rearrange("p (k n) -> p k n", k=KB),
                               ins[f"up{layer}"][:, f0:f0 + cols].rearrange("(k p) n -> p k n", p=P)),
                        "down": (stage[0:width, 2048:2048 + tiles * CH].rearrange("p (k n) -> p k n", k=tiles),
                                 ins[f"down{layer}"][f0:f0 + cols, :].rearrange("(k p) n -> p k n", p=width)),
                    }
                    for dst, src in srcs.values():
                        w_loads[1] += 16
                        sync.quiet(lambda e, dst=dst, src=src: e.dma_start(dst, src).then_inc(w_loads[0], 16),
                                   stage_free[0])
                    box["in"] = (w_loads[0], w_loads[1])

                work = [bring]
                for i, name in enumerate(("gate", "up", "down")):
                    rows = width if name == "down" else P
                    n_cols = tiles * CH if name == "down" else KB * cols

                    def cut(which, i=i, name=name, rows=rows, n_cols=n_cols):
                        src = stage[0:rows, i * 1024:i * 1024 + n_cols]
                        hi, lo = (p[0:rows, box["slot"], 0:n_cols] for p in parts[name])
                        if which == 0:
                            box["t"] = pool(lambda e: copy_on_pool(e, hi, src), box["in"], box["free"], start)
                        else:
                            box["t"] = pool(lambda e: e.tensor_tensor(lo, src, hi.bitcast(F32), ALU.subtract),
                                            box["t"])
                            w_state[n, name] = (box["slot"], box["t"])
                            if name == "down":
                                stage_free[0] = box["t"]

                    work += [lambda c=cut: c(0), lambda c=cut: c(1)]
                return work

            for w in weight_work(0):
                w()

            xt_done = []
            for c in range(4):
                cols = slice(c * 512, (c + 1) * 512)
                xt_done.append(to_channels(lambda i, c=c: x[:, 4 * c + i, :], xt_hi[:, :, cols],
                                           xt_lo[:, :, cols], x_ready[c], start))

            banks = Ring(2)
            for slot in range(2):
                banks.give(slot, *pairs.readers)
            ROUTER_BANKS = (2 * BANK, 5 * BANK)
            logits = buf("logits", [P, ALL_TILES, E])
            logits_t = buf("logits_t", [E, T])

            def logits_known():
                read = [pairs.readers[:], pairs.readers[:]]
                for c in range(4):
                    base = ROUTER_BANKS[c % 2]
                    todo = products(psum[0:E, base:base + 512], [(gw_hi[:, k, :], gw_lo[:, k, :]) for k in range(KB)],
                                    [(xt_hi[:, k, c * 512:(c + 1) * 512], xt_lo[:, k, c * 512:(c + 1) * 512])
                                     for k in range(KB)])
                    for mm in todo[:-1]:
                        pe.quiet(mm, xt_done[c], read[c % 2], gw_ready)
                    lg = pe(todo[-1])
                    read[c % 2] = act(lambda e, c=c, base=base: e.activation(
                        logits_t[:, c * 512:(c + 1) * 512], psum[0:E, base:base + 512], ACT.Copy), lg, start)
                yield
                for t in range(ALL_TILES):
                    base = ROUTER_BANKS[0] + t * E
                    tr = pe(lambda e, t=t, base=base: e.transpose(
                        psum[:, base:base + E], logits_t[:, t * P:(t + 1) * P], ident[0:E, 0:E]), read)
                lg_out = dve(lambda e: e.tensor_copy(
                    logits[:], psum[:, ROUTER_BANKS[0]:ROUTER_BANKS[0] + ALL_TILES * E].rearrange(
                        "p (t n) -> p t n", n=E)), tr, start)
                yield
                return lg_out

            if E == 2:
                top = buf("top", [P, ALL_TILES])
                prob = buf("prob", [P, ALL_TILES, E])
                tot = buf("tot", [P, ALL_TILES])
                is_top = buf("is_top", [P, ALL_TILES, E])
                coef = buf("coef", [P, ALL_TILES, E])
                l0, l1 = logits[:, :, 0], logits[:, :, 1]
                coef_ready = []

                def gating():
                    lg_out = yield from logits_known()
                    r = dve(lambda e: e.tensor_tensor(top[:], l0, l1, ALU.max), lg_out)
                    r = dve(lambda e: e.tensor_tensor(prob[:], logits[:], top[:].unsqueeze(2).to_broadcast(
                        [P, ALL_TILES, E]), ALU.subtract), r)
                    r = act(lambda e: e.activation(prob[:], prob[:], ACT.Exp), r)
                    r = dve(lambda e: e.tensor_tensor(tot[:], prob[:, :, 0], prob[:, :, 1], ALU.add), r)
                    r = dve(lambda e: e.reciprocal(tot[:], tot[:]), r)
                    r = dve(lambda e: e.tensor_tensor(prob[:], prob[:], tot[:].unsqueeze(2).to_broadcast(
                        [P, ALL_TILES, E]), ALU.mult), r)
                    dve(lambda e: e.tensor_tensor(is_top[:, :, 0], prob[:, :, 0], prob[:, :, 1], ALU.is_ge), r)
                    r = dve(lambda e: e.tensor_tensor(is_top[:, :, 1], prob[:, :, 1], prob[:, :, 0], ALU.is_gt), r)
                    coef_ready.append(dve(lambda e: e.tensor_tensor(coef[:], prob[:], is_top[:], ALU.mult), r))
            else:
                TOP_K = 6
                score = buf("score", [P, ALL_TILES, E + 8 - TOP_K])
                best = buf("best", [P, ALL_TILES, 8])
                rest = buf("rest", [P, ALL_TILES, E + 8 - TOP_K])
                tot = buf("tot", [P, ALL_TILES])
                comb = buf("comb", [P, ALL_TILES, E])
                comb_rows = buf("comb_rows", [P, ALL_TILES, P], F32R)
                comb_t = buf("comb_t", [P, T], F32R)
                F = groups[0][0]
                pick_f = buf("pick_f", [P, F], F32R)
                sc = score[:, :, 0:E]
                dve(lambda e: e.memset(score[:], -1.0), start)
                cleared = dve(lambda e: e.memset(comb_rows[:].bitcast(F32), 0.0), start)
                pick_raw = buf("pick_raw", [2 * E, F])
                pick_in = load("pick_f", pick_raw[:], ins["pick_f"], start)
                pick_set = act(lambda e: e.activation(pick_f[0:2 * E, :], pick_raw[:], ACT.Copy), pick_in)
                pick_clear = zero(pick_f[2 * E:P, :], start)

                def gating():
                    lg_out = yield from logits_known()
                    r = act(lambda e: e.activation(logits[:], logits[:], ACT.Exp, scale=-1.0), lg_out)
                    r = dve(lambda e: e.tensor_scalar(logits[:], logits[:], 1.0, None, ALU.add), r)
                    scored = dve(lambda e: e.reciprocal(sc, logits[:]), r)
                    yield
                    for t in range(ALL_TILES):
                        b8 = dve(lambda e, t=t: e.max(best[:, t, :], score[:, t, 0:E]), scored)
                        if t % 8 == 7:
                            yield
                    low = dve(lambda e: e.memset(best[:, :, TOP_K:8], -1.0), b8)
                    for t in range(ALL_TILES):
                        mr = dve(lambda e, t=t: e.match_replace(rest[:, t, :], best[:, t, :], score[:, t, :],
                                                                -2.0), low)
                        if t % 8 == 7:
                            yield
                    r = dve(lambda e: e.tensor_tensor(comb[:], rest[:, :, 0:E], sc, ALU.not_equal), mr)
                    r = dve(lambda e: e.tensor_tensor(comb[:], comb[:], sc, ALU.mult), r)
                    r = dve(lambda e: e.tensor_reduce(tot[:], comb[:], X_AXIS, ALU.add), r)
                    yield
                    r = dve(lambda e: e.tensor_scalar(tot[:], tot[:], 1e-20, None, ALU.add), r)
                    r = dve(lambda e: e.reciprocal(tot[:], tot[:]), r)
                    r = dve(lambda e: e.tensor_tensor(comb[:], comb[:], tot[:].unsqueeze(2).to_broadcast(
                        [P, ALL_TILES, E]), ALU.mult), r)
                    r = dve(lambda e: e.tensor_copy(comb_rows[:, :, 0:E], comb[:]), r, cleared)
                    r = dve(lambda e: e.tensor_tensor(comb_rows[:, :, E:2 * E], comb[:],
                                                      comb_rows[:, :, 0:E].bitcast(F32), ALU.subtract), r)
                    yield
                    free = [banks.readers[0], banks.readers[1]]
                    for c in range(4):
                        bank = (2 + 3 * (c % 2)) * BANK
                        for i in range(4):
                            tr = (lambda e, i=i, c=c, bank=bank: e.transpose(
                                psum[:, bank + i * P:bank + (i + 1) * P],
                                comb_rows[:, 4 * c + i, :].bitcast(F32), ident[:]))
                            if i == 3:
                                turned = pe(tr)
                            else:
                                pe.quiet(tr, r, comb_done[c - 2] if c > 1 else free)
                        comb_done.append(act(lambda e, c=c, bank=bank: e.activation(
                            comb_t[:, c * 512:(c + 1) * 512], psum[:, bank:bank + 512], ACT.Copy), turned))

                comb_done = []

            OUT = 6 * BANK
            out_free = [list(flat(o_read + pairs.readers))]
            bufs = Ring(2)
            pending = []
            work = []
            laid_anew = []

            def down(item):
                n, c, j, slot, hi_ready, lo_ready = item
                f0, width, tiles, kind = groups[n]
                w_slot, w_ready = w_state[n, "down"]
                w_hi, w_lo = (p[0:width, w_slot, j * CH:(j + 1) * CH] for p in parts["down"])
                first, last = j == 0, j == tiles - 1
                for a, w, ready in ((hid_hi, w_hi, hi_ready), (hid_hi, w_lo, hi_ready), (hid_lo, w_hi, lo_ready)):
                    for i in range(4):
                        opens = first and w is w_hi and a is hid_hi and i % 2 == 0
                        closes = last and a is hid_lo
                        mm = (lambda e, a=a, w=w, i=i, opens=opens, closes=closes: e.matmul(
                            psum[:, OUT + i * CH:OUT + (i + 1) * CH], a[0:width, slot, i * P:(i + 1) * P], w,
                            start=opens, stop=closes, skip_group_check=True))
                        if a is hid_lo and i == 3:
                            done = pe(mm)
                        else:
                            pe.quiet(mm, ready, w_ready, out_free[0] if first else None)
                bufs.give(slot, done)
                if last:
                    if c == 3:
                        w_free.give(w_slot, done)
                    xs = x[:, 4 * c:4 * c + 4, :]
                    if kind[0] == "scaled":
                        for i in range(4):
                            t = 4 * c + i
                            added = dve(lambda e, i=i, t=t: e.scalar_tensor_tensor(
                                x[:, t, :], psum[:, OUT + i * CH:OUT + (i + 1) * CH], coef[:, t, kind[1]:kind[1] + 1],
                                x[:, t, :], ALU.mult, ALU.add), done, coef_ready, x_ready[c])
                    else:
                        added = dve(lambda e: e.tensor_tensor(
                            xs.rearrange("p t n -> p (t n)"), psum[:, OUT:OUT + 1024],
                            xs.rearrange("p t n -> p (t n)"), ALU.add), done, x_ready[c])
                    out_free[0] = added
                    x_ready[c] = added
                    if n == len(groups) - 1:
                        laid_anew[:] = fence()
                        norm_parts = normalizing(c, added)
                        work.extend([lambda: next(norm_parts, None)] * 3)

            for n, (f0, width, tiles, kind) in enumerate(groups):
                gating_parts = gating() if n == 0 else None
                work += weight_work(n + 1) if n + 1 < len(groups) else []
                for c in range(4):
                    cols = slice(c * 512, (c + 1) * 512)
                    for j in range(tiles):
                        slot, free = banks.take()
                        b_slot, b_free = bufs.take()
                        base = slot * 3 * BANK
                        w_slot = w_state[n, "gate"][0]

                        def weights(name, k):
                            at = k * width * tiles + j * width
                            return tuple(p[:, w_slot, at:at + width] for p in parts[name])

                        rhs = [(xt_hi[:, k, cols], xt_lo[:, k, cols]) for k in range(KB)]
                        done = []
                        for i, name in enumerate(("gate", "up")):
                            todo = products(psum[0:width, base + i * BANK:base + (i + 1) * BANK],
                                            [weights(name, k) for k in range(KB)], rhs)
                            for mm in todo[:-1]:
                                pe.quiet(mm, free, w_state[n, name][1], xt_done[c])
                            done.append(pe(todo[-1]))
                        g_ps, u_ps, c_ps = (psum[0:width, base + i * BANK:base + (i + 1) * BANK] for i in range(3))
                        sg, hd = silu[0:width, b_slot, :], hid[0:width, b_slot, :]
                        hh, hl = hid_hi[0:width, b_slot, :], hid_lo[0:width, b_slot, :]
                        r = act(lambda e, sg=sg, g_ps=g_ps: e.activation(sg, g_ps, ACT.Silu), done[0], b_free, start)
                        if kind[0] == "routed":
                            fs = slice(f0 + j * width, f0 + (j + 1) * width)
                            mix = pe(lambda e, c_ps=c_ps, fs=fs, cols=cols: e.matmul(
                                c_ps, pick_f[:, fs], comb_t[:, cols], start=True, stop=True), comb_done, pick_set, pick_clear)
                            r = dve(lambda e, sg=sg, c_ps=c_ps: e.tensor_tensor(sg, c_ps, sg, ALU.mult), r, mix)
                        r = dve(lambda e, hd=hd, sg=sg, u_ps=u_ps: e.tensor_tensor(hd, u_ps, sg, ALU.mult),
                                r, done[1], b_free)
                        banks.give(slot, r)
                        hi = act(lambda e, hh=hh, hd=hd: e.activation(hh, hd, ACT.Copy), r, b_free)
                        lo = pool(lambda e, hh=hh, hd=hd, hl=hl: e.tensor_tensor(hl, hd, hh.bitcast(F32),
                                                                                 ALU.subtract), hi)
                        while pending:
                            down(pending.pop())
                        if work:
                            work.pop(0)()
                        if gating_parts:
                            next(gating_parts, None)
                        pending.append((n, c, j, b_slot, hi, lo))
                while work and n < len(groups) - 1:
                    work.pop(0)()
                if gating_parts:
                    for _ in gating_parts:
                        pass
            while pending:
                down(pending.pop())
            while work:
                work.pop(0)()
            pairs.readers[:] = [[(pe.sem, pe.count), (dve.sem, dve.count)]] * 3
            o_read[:] = [[(pe.sem, pe.count), (dve.sem, dve.count)]] * 2
            s.close()
            return laid_anew

        free = attention(0, AttentionShape(16, softmax=False), None)
        free = experts(0, free, [(512 * n, P, 4, ("scaled", n // 2)) for n in range(4)], 2)
        free = attention(1, AttentionShape(32, softmax=True), free)
        experts(1, free, [(3072, 96, 2, ("plain",))] + [(512 * n, P, 4, ("routed",)) for n in range(6)], 32)

        stored = sem("stored")
        for c in range(ALL_TILES // 4):
            sync.quiet(lambda e, c=c: e.dma_start(out_dram[:, 4 * c:4 * c + 4, :],
                                                  x[:, 4 * c:4 * c + 4, :]).then_inc(stored, 16), x_ready[c])

        block = ctx.enter_context(nc.Block())

        @block.sync
        def _(eng):
            sync.play(eng)
            eng.wait_ge(stored, 16 * (ALL_TILES // 4))

        block.tensor(pe.play)
        block.scalar(act.play)
        block.vector(dve.play)
        block.gpsimd(pool.play)


def rope_tables(base_freqs, angles, scale):
    c = np.cos(angles.astype(np.float64))
    s = np.sin(angles.astype(np.float64))
    cos = np.concatenate([c, c], -1)
    sin = np.concatenate([-s, s], -1)
    both = [np.stack([t * scale, t], 1).astype(np.float32) for t in (cos, sin)]
    return [np.ascontiguousarray(t.reshape(TILES, P, 2, -1).transpose(1, 0, 2, 3)) for t in both]


def constants(n_experts, expert_width):
    f32 = np.float32
    d0, d1 = CH // 16, CH // 32
    t = np.arange(SEQ, dtype=f32)
    inv0 = (1.0 / f32(10000.0) ** (np.arange(0, d0, 2, dtype=f32) / f32(d0))).astype(f32)
    cos0, sin0 = rope_tables(inv0, t[:, None] * inv0[None, :], 1.0)
    theta = (f32(10000.0) ** (-np.arange(0, d1, 2, dtype=f32) / f32(d1))).astype(f32)
    temporal = np.floor((np.arange(SEQ) // 72).astype(f32) * 0.5).astype(f32)
    angles = (t[:, None] * theta).astype(np.float64) + (temporal[:, None] * theta).astype(np.float64)
    cos1, sin1 = rope_tables(theta, angles, 1.0 / np.sqrt(d1))
    i = np.arange(P)
    return {
        "ident": np.eye(P, dtype=f32),
        "later": np.stack([np.where(i[None, :] > i[:, None], f32(MASKED), f32(0)),
                           np.where(i[None, :] < i[:, None], f32(MASKED), f32(0))], 1),
        "pick": np.eye(2, dtype=f32),
        "pick_f": np.tile(np.repeat(np.eye(n_experts, dtype=f32), expert_width, axis=1), (2, 1)),
        "cos0": cos0, "sin0": sin0, "cos1": cos1, "sin1": sin1,
    }


def kernel(**inputs):
    import concourse.bacc as bacc
    from concourse.bass_utils import run_bass_kernel_spmd

    a = {k: np.asarray(v) for k, v in inputs.items()}
    width = a["L1_ffn_wd"].shape[0] * a["L1_ffn_wd"].shape[1]

    def by_channel(w):
        return w.transpose(1, 0, 2).reshape(CH, -1)

    arrays = {
        "x": a["L0_attn_x"],
        "wqkv0": a["L0_attn_w_qkv"], "wo0": a["L0_attn_w_out"],
        "ln_scale": a["L0_attn_ln_scale"], "ln_bias": a["L0_attn_ln_bias"],
        "router0": a["L0_ffn_gate_w"].T,
        "gate0": by_channel(a["L0_ffn_w_gate"].transpose(0, 2, 1)),
        "up0": by_channel(a["L0_ffn_w_up"].transpose(0, 2, 1)),
        "down0": a["L0_ffn_w_down"].transpose(0, 2, 1).reshape(-1, CH),
        "wqkv1": np.concatenate([a["L1_attn_Wq"].T, a["L1_attn_Wk"].T, a["L1_attn_Wv"].T], 1),
        "wo1": a["L1_attn_Wo"].T,
        "bias": np.concatenate([a["L1_attn_bq"], a["L1_attn_bk"], a["L1_attn_bv"], a["L1_attn_bo"]]),
        "router1": a["L1_ffn_gate_w"],
        "gate1": np.concatenate([by_channel(a["L1_ffn_wg"]), a["L1_ffn_sg"]], 1),
        "up1": np.concatenate([by_channel(a["L1_ffn_wu"]), a["L1_ffn_su"]], 1),
        "down1": np.concatenate([a["L1_ffn_wd"].reshape(width, CH), a["L1_ffn_sd"]], 0),
        **constants(*a["L1_ffn_wg"].shape[0::2]),
    }
    nc = bacc.Bacc("TRN2", target_bir_lowering=False, num_devices=1)
    feeds, ins = {}, {}
    for name, value in arrays.items():
        value = np.ascontiguousarray(value)
        feeds[f"in_{name}"] = value
        ins[name] = nc.dram_tensor(f"in_{name}", value.shape, mybir.dt.from_np(value.dtype),
                                   kind="ExternalInput").ap()
    out = nc.dram_tensor("out", (BATCH, SEQ, CH), F32, kind="ExternalOutput").ap()
    build_program(nc, ins, out)
    result = run_bass_kernel_spmd(nc, [feeds], core_ids=[0])
    return result.results[0]["out"]
```
